# Optimizing a Trainium2 kernel written in Bass

```python
import numpy as np
import jax
import jax.numpy as jnp

def _softmax(x, axis=-1):
    return jax.nn.softmax(x, axis=axis)

def _gelu(x):
    return jax.nn.gelu(x, approximate=True)

def _silu(x):
    return jax.nn.silu(x)

def _sigmoid(x):
    return jax.nn.sigmoid(x)

def _layernorm(x, axis=-1, eps=1e-05):
    m = jnp.mean(x, axis=axis, keepdims=True)
    v = jnp.var(x, axis=axis, keepdims=True)
    return (x - m) / jnp.sqrt(v + eps)

def _scatter_add(tgt, idx, src, axis=0):
    return tgt.at[idx].add(src)

def _segment_sum(src, seg, n):
    return jax.ops.segment_sum(src, seg, n)
kernel_name = 'mk_flamingo_gated_d2_seqx_r4_1c9842'

def setup_inputs(seed: int=0):
    np.random.seed(seed)
    _w = jnp.asarray

    def _rec_inputs():
        import jax
        import jax.numpy as jnp
        _rk = jax.random.key(seed)
        x = 7.22e-05 + 1 * jax.random.normal(jax.random.fold_in(_rk, 1), (16, 256, 256), jnp.float32)
        _lenS = 256 - jax.random.randint(jax.random.fold_in(_rk, 7), (16,), 0, max(1, 256 // 4) + 1, jnp.int32)
        _lenS2 = 256 - jax.random.randint(jax.random.fold_in(_rk, 8), (16,), 0, max(1, 256 // 4) + 1, jnp.int32)
        _ctx_1024P = jax.random.normal(jax.random.fold_in(_rk, 11), (16, 16, 256), jnp.float32)
        _ctx_1024c = jax.random.dirichlet(jax.random.fold_in(_rk, 511), 0.3 * jnp.ones((16,), jnp.float32), (16, 256))
        _ctx_1024t = jnp.einsum('bsk,bkd->bsd', _ctx_1024c, _ctx_1024P)
        _ctx_1024t = _ctx_1024t * jax.lax.rsqrt(jnp.mean(jnp.square(_ctx_1024t)) + 1e-12) * 0.953939
        ctx_1024 = 4.13588e-05 + 0.999923 * (_ctx_1024t + 0.3 * jax.random.normal(jax.random.fold_in(_rk, 611), (16, 256, 256), jnp.float32))
        _validS = jnp.arange(256)[None, :] < _lenS[:, None]
        _validS2 = jnp.arange(256)[None, :] < _lenS2[:, None]
        _causal = jnp.tril(jnp.ones((256, 256), dtype=bool))
        mask_Bx1xSxS2_bk0 = jnp.logical_not(jnp.broadcast_to(_validS2[:, None, None, :], (16, 1, 256, 256)))
        mask_BxS2_if0 = jnp.where(jnp.ones((16, 256), dtype=bool), 0, 1).astype(jnp.int32)
        _g = jax.random.normal(jax.random.fold_in(_rk, 9001), (2, 2), jnp.float32)
        _g = jnp.sign(_g) * jnp.maximum(jnp.abs(_g), 1.0) + (_g == 0) * 1.0
        g_xattn = _g[0]
        g_ffn = _g[1]
        return (x, ctx_1024, mask_Bx1xSxS2_bk0, mask_BxS2_if0, g_xattn, g_ffn)
    x, ctx_1024, mask_Bx1xSxS2_bk0, mask_BxS2_if0, g_xattn, g_ffn = _rec_inputs()

    def _L0_xattn_setup():
        import jax, jax.numpy as jnp
        import numpy as np
        D_MODEL = 256
        N_HEADS = 16
        D_HEAD = D_MODEL // N_HEADS
        B = 4
        S = 512
        NEG_INF = -10000000000.0
        key = jax.random.key(seed)
        ks = jax.random.split(key, 8)
        queries = jax.random.normal(ks[0], (B, S, D_MODEL), dtype=jnp.float32)
        keys = jax.random.normal(ks[1], (B, S, D_MODEL), dtype=jnp.float32)
        values = jax.random.normal(ks[2], (B, S, D_MODEL), dtype=jnp.float32)
        causal = jnp.tril(jnp.ones((S, S), dtype=bool))
        mask = jnp.broadcast_to(causal[None, None, :, :], (B, 1, S, S))
        sc = 1.0 / np.sqrt(D_MODEL)
        W_q = jax.random.normal(ks[3], (D_MODEL, D_MODEL), dtype=jnp.float32) * sc
        W_k = jax.random.normal(ks[4], (D_MODEL, D_MODEL), dtype=jnp.float32) * sc
        W_v = jax.random.normal(ks[5], (D_MODEL, D_MODEL), dtype=jnp.float32) * sc
        W_proj = jax.random.normal(ks[6], (D_MODEL, D_MODEL), dtype=jnp.float32) * sc
        b_proj = jnp.zeros((D_MODEL,), dtype=jnp.float32)
        return {'queries': queries, 'keys': keys, 'values': values, 'mask': mask, 'W_q': W_q, 'W_k': W_k, 'W_v': W_v, 'W_proj': W_proj, 'b_proj': b_proj}
    _L0_xattn_all = _L0_xattn_setup()
    _L0_xattn_in = {k: v for k, v in _L0_xattn_all.items() if k in ('W_q', 'W_k', 'W_v', 'W_proj', 'b_proj')}
    del _L0_xattn_all

    def _L0_ffn_setup():
        import jax, jax.numpy as jnp
        import numpy as np
        BLOCK = 32
        W_BITS = 4
        ACT_BITS = 16

        def act_qdq(x):
            qmax = 2.0 ** (ACT_BITS - 1) - 1.0
            scale = jnp.maximum(jnp.max(jnp.abs(x)) / qmax, 1e-12)
            return jnp.clip(jnp.round(x / scale), -qmax - 1.0, qmax) * scale

        def fixed_qdq_u16(x):
            scale = 1.0 / 65536.0
            return jnp.clip(jnp.round(x / scale), 0.0, 65535.0) * scale

        def lpbq_dequant(w):
            O, I = w.shape
            qmax = 2.0 ** (W_BITS - 1) - 1.0
            wb = w.reshape(O, I // BLOCK, BLOCK)
            s = jnp.maximum(jnp.max(jnp.abs(wb), axis=-1, keepdims=True) / qmax, 1e-12)
            wq = jnp.clip(jnp.round(wb / s), -qmax - 1.0, qmax) * s
            return wq.reshape(O, I)
        key = jax.random.key(seed)
        k1, k2, k3, k4 = jax.random.split(key, 4)
        B, S, H, I = (2, 1024, 256, 768)
        x = jax.random.normal(k1, (B, S, H), jnp.float32)
        w_gate = jax.random.normal(k2, (I, H), jnp.float32) * 0.02
        w_up = jax.random.normal(k3, (I, H), jnp.float32) * 0.02
        w_down = jax.random.normal(k4, (H, I), jnp.float32) * 0.02
        return {'x': x, 'w_gate': w_gate, 'w_up': w_up, 'w_down': w_down}
    _L0_ffn_all = _L0_ffn_setup()
    _L0_ffn_in = {k: v for k, v in _L0_ffn_all.items() if k in ('w_gate', 'w_up', 'w_down')}
    del _L0_ffn_all

    def _L1_xattn_setup():
        import jax, jax.numpy as jnp
        import numpy as np
        DIM = 256
        HEADS = 16
        HEAD_DIM = DIM // HEADS
        B, NQ, NK = (2, 512, 512)
        key = jax.random.key(seed)
        ks = jax.random.split(key, 8)
        s = 1.0 / np.sqrt(DIM)
        return {'query': jax.random.normal(ks[0], (B, NQ, DIM), jnp.float32), 'key': jax.random.normal(ks[1], (B, NK, DIM), jnp.float32), 'value': jax.random.normal(ks[2], (B, NK, DIM), jnp.float32), 'qpos': jnp.zeros((B, NQ), jnp.int32), 'kpos': jnp.zeros((B, NK), jnp.int32), 'Wq': jax.random.normal(ks[3], (DIM, DIM), jnp.float32) * s, 'Wk': jax.random.normal(ks[4], (DIM, DIM), jnp.float32) * s, 'Wv': jax.random.normal(ks[5], (DIM, DIM), jnp.float32) * s, 'Wo': jax.random.normal(ks[6], (DIM, DIM), jnp.float32) * s, 'bo': jax.random.normal(ks[7], (DIM,), jnp.float32) * s}
    _L1_xattn_all = _L1_xattn_setup()
    _L1_xattn_in = {k: v for k, v in _L1_xattn_all.items() if k in ('Wq', 'Wk', 'Wv', 'Wo', 'bo')}
    del _L1_xattn_all

    def _L1_ffn_setup():
        import math
        import jax, jax.numpy as jnp
        import numpy as np
        CAPACITY_FACTOR = 1.25
        key = jax.random.key(seed)
        ks = jax.random.split(key, 5)
        B, S, H, F, E = (4, 1024, 256, 256, 32)
        scale_in = 1.0 / math.sqrt(H)
        scale_mid = 1.0 / math.sqrt(F)
        return {'x': jax.random.normal(ks[0], (B, S, H), dtype=jnp.float32), 'w_router': jax.random.normal(ks[1], (H, E), dtype=jnp.float32) * scale_in, 'w_gate': jax.random.normal(ks[2], (E, H, F), dtype=jnp.float32) * scale_in, 'w_up': jax.random.normal(ks[3], (E, H, F), dtype=jnp.float32) * scale_in, 'w_down': jax.random.normal(ks[4], (E, F, H), dtype=jnp.float32) * scale_mid}
    _L1_ffn_all = _L1_ffn_setup()
    _L1_ffn_in = {k: v for k, v in _L1_ffn_all.items() if k in ('w_router', 'w_gate', 'w_up', 'w_down')}
    del _L1_ffn_all
    return {'x': x, 'ctx_1024': ctx_1024, 'mask_Bx1xSxS2_bk0': mask_Bx1xSxS2_bk0, 'mask_BxS2_if0': mask_BxS2_if0, 'g_xattn': g_xattn, 'g_ffn': g_ffn, 'L0_xattn_W_q': _L0_xattn_in['W_q'], 'L0_xattn_W_k': _L0_xattn_in['W_k'], 'L0_xattn_W_v': _L0_xattn_in['W_v'], 'L0_xattn_W_proj': _L0_xattn_in['W_proj'], 'L0_xattn_b_proj': _L0_xattn_in['b_proj'], 'L0_ffn_w_gate': _L0_ffn_in['w_gate'], 'L0_ffn_w_up': _L0_ffn_in['w_up'], 'L0_ffn_w_down': _L0_ffn_in['w_down'], 'L1_xattn_Wq': _L1_xattn_in['Wq'], 'L1_xattn_Wk': _L1_xattn_in['Wk'], 'L1_xattn_Wv': _L1_xattn_in['Wv'], 'L1_xattn_Wo': _L1_xattn_in['Wo'], 'L1_xattn_bo': _L1_xattn_in['bo'], 'L1_ffn_w_router': _L1_ffn_in['w_router'], 'L1_ffn_w_gate': _L1_ffn_in['w_gate'], 'L1_ffn_w_up': _L1_ffn_in['w_up'], 'L1_ffn_w_down': _L1_ffn_in['w_down']}

def reference(x, ctx_1024, mask_Bx1xSxS2_bk0, mask_BxS2_if0, g_xattn, g_ffn, L0_xattn_W_q, L0_xattn_W_k, L0_xattn_W_v, L0_xattn_W_proj, L0_xattn_b_proj, L0_ffn_w_gate, L0_ffn_w_up, L0_ffn_w_down, L1_xattn_Wq, L1_xattn_Wk, L1_xattn_Wv, L1_xattn_Wo, L1_xattn_bo, L1_ffn_w_router, L1_ffn_w_gate, L1_ffn_w_up, L1_ffn_w_down):
    import jax
    import jax.numpy as jnp

    def _L0_xattn_ref(queries, keys, values, mask, W_q, W_k, W_v, W_proj, b_proj):
        import jax, jax.numpy as jnp
        import numpy as np
        D_MODEL = 256
        N_HEADS = 16
        D_HEAD = D_MODEL // N_HEADS
        B = 4
        S = 512
        NEG_INF = -10000000000.0
        b, sq, _ = queries.shape
        Q = (queries @ W_q.T).reshape(b, sq, N_HEADS, D_HEAD).transpose(0, 2, 1, 3)
        K = (keys @ W_k.T).reshape(b, -1, N_HEADS, D_HEAD).transpose(0, 2, 1, 3)
        V = (values @ W_v.T).reshape(b, -1, N_HEADS, D_HEAD).transpose(0, 2, 1, 3)
        scale = jnp.sqrt(jnp.float32(D_HEAD))
        scores = jnp.einsum('bhqd,bhkd->bhqk', Q, K) / scale
        scores = jnp.where(mask, scores, NEG_INF)
        attention = jax.nn.softmax(scores, axis=-1)
        heads_out = jnp.einsum('bhqk,bhkd->bhqd', attention, V)
        heads_out = heads_out.transpose(0, 2, 1, 3).reshape(b, sq, D_MODEL)
        out = heads_out @ W_proj.T + b_proj
        return out

    def _L0_ffn_ref(x, w_gate, w_up, w_down):
        import jax, jax.numpy as jnp
        import numpy as np
        BLOCK = 32
        W_BITS = 4
        ACT_BITS = 16

        def act_qdq(x):
            qmax = 2.0 ** (ACT_BITS - 1) - 1.0
            scale = jnp.maximum(jnp.max(jnp.abs(x)) / qmax, 1e-12)
            return jnp.clip(jnp.round(x / scale), -qmax - 1.0, qmax) * scale

        def fixed_qdq_u16(x):
            scale = 1.0 / 65536.0
            return jnp.clip(jnp.round(x / scale), 0.0, 65535.0) * scale

        def lpbq_dequant(w):
            O, I = w.shape
            qmax = 2.0 ** (W_BITS - 1) - 1.0
            wb = w.reshape(O, I // BLOCK, BLOCK)
            s = jnp.maximum(jnp.max(jnp.abs(wb), axis=-1, keepdims=True) / qmax, 1e-12)
            wq = jnp.clip(jnp.round(wb / s), -qmax - 1.0, qmax) * s
            return wq.reshape(O, I)
        x = act_qdq(x)
        up = act_qdq(x @ lpbq_dequant(w_up).T)
        gate = act_qdq(x @ lpbq_dequant(w_gate).T)
        sig = fixed_qdq_u16(jax.nn.sigmoid(gate))
        gate = act_qdq(gate * sig)
        o = act_qdq(gate * up)
        return o @ lpbq_dequant(w_down).T

    def _L1_xattn_ref(query, key, value, qpos, kpos, Wq, Wk, Wv, Wo, bo):
        import jax, jax.numpy as jnp
        import numpy as np
        DIM = 256
        HEADS = 16
        HEAD_DIM = DIM // HEADS
        B, NQ, NK = (2, 512, 512)
        Bq, Nq, C = query.shape
        Nk = key.shape[1]
        scale = HEAD_DIM ** (-0.5)
        q = (query @ Wq.T).reshape(Bq, Nq, HEADS, HEAD_DIM).transpose(0, 2, 1, 3)
        k = (key @ Wk.T).reshape(Bq, Nk, HEADS, HEAD_DIM).transpose(0, 2, 1, 3)
        v = (value @ Wv.T).reshape(Bq, Nk, HEADS, HEAD_DIM).transpose(0, 2, 1, 3)
        attn = jnp.einsum('bhqd,bhkd->bhqk', q, k) * scale
        attn = jax.nn.softmax(attn, axis=-1)
        x = jnp.einsum('bhqk,bhkd->bhqd', attn, v)
        x = x.transpose(0, 2, 1, 3).reshape(Bq, Nq, C)
        return x @ Wo.T + bo

    def _L1_ffn_ref(x, w_router, w_gate, w_up, w_down):
        import math
        import jax, jax.numpy as jnp
        import numpy as np
        CAPACITY_FACTOR = 1.25
        B, S, H = x.shape
        E = w_gate.shape[0]
        T = B * S
        C = int(math.ceil(CAPACITY_FACTOR * T / E))
        xt = x.reshape(T, H)
        logits = xt @ w_router
        probs = jax.nn.softmax(logits, axis=-1)
        top1 = jnp.argmax(probs, axis=-1)
        gate = jnp.take_along_axis(probs, top1[:, None], axis=1)[:, 0]
        onehot = jax.nn.one_hot(top1, E, dtype=jnp.int32)
        pos = jnp.cumsum(onehot, axis=0)[jnp.arange(T), top1] - 1
        accepted = pos < C
        slot = jnp.where(accepted, top1 * C + pos, E * C)
        buf = jnp.zeros((E * C + 1, H), dtype=x.dtype).at[slot].set(xt)
        buf = buf[:E * C].reshape(E, C, H)
        g = jnp.einsum('ech,ehf->ecf', buf, w_gate)
        u = jnp.einsum('ech,ehf->ecf', buf, w_up)
        y = jnp.einsum('ecf,efh->ech', jax.nn.silu(g) * u, w_down)
        out_tok = y.reshape(E * C, H)[jnp.clip(slot, 0, E * C - 1)]
        out_tok = jnp.where(accepted[:, None], out_tok * gate[:, None], 0.0)
        return (xt + out_tok).reshape(B, S, H)
    x = x + jnp.tanh(g_xattn[0]) * _L0_xattn_ref(_layernorm(x, axis=-1), ctx_1024, ctx_1024, mask_Bx1xSxS2_bk0, L0_xattn_W_q, L0_xattn_W_k, L0_xattn_W_v, L0_xattn_W_proj, L0_xattn_b_proj)
    x = x + jnp.tanh(g_ffn[0]) * _L0_ffn_ref(_layernorm(x, axis=-1), L0_ffn_w_gate, L0_ffn_w_up, L0_ffn_w_down)
    x = x + jnp.tanh(g_xattn[1]) * _L1_xattn_ref(_layernorm(x, axis=-1), ctx_1024, ctx_1024, mask_BxS2_if0, mask_BxS2_if0, L1_xattn_Wq, L1_xattn_Wk, L1_xattn_Wv, L1_xattn_Wo, L1_xattn_bo)
    x = x + jnp.tanh(g_ffn[1]) * _L1_ffn_ref(_layernorm(x, axis=-1), L1_ffn_w_router, L1_ffn_w_gate, L1_ffn_w_up, L1_ffn_w_down)
    return x

_drawn_inputs = setup_inputs


def setup_inputs(seed=0):
    import zlib

    import numpy as np

    out = dict(_drawn_inputs(seed))
    spreads = {'g_ffn': (-1.0, 0.2), 'L0_xattn_b_proj': (0.0, 0.1)}
    factors = {}
    for name, (base, spread) in spreads.items():
        noise = np.random.default_rng([zlib.crc32(name.encode()), seed]).standard_normal(out[name].shape)
        drawn = base * np.exp(spread * noise) if base else spread * noise
        out[name] = jnp.asarray(drawn.astype(out[name].dtype))
    for name, factor in factors.items():
        out[name] = (out[name] * factor).astype(out[name].dtype)
    return out
```

```python
from contextlib import ExitStack

import numpy as np
import concourse.bass as bass
from concourse import mybir

F32 = mybir.dt.float32
BF16 = mybir.dt.bfloat16
I16 = mybir.dt.int16
U16 = mybir.dt.uint16
I32 = mybir.dt.int32
U8 = mybir.dt.uint8
ALU = mybir.AluOpType
ACT = mybir.ActivationFunctionType
X = mybir.AxisListType.X

NB, S, D, H, HD = 16, 256, 256, 16, 16
T = NB * S
FF = 768
E, C = 32, 160
EC = E * C
NEG = -1.0e10
EPS = 1e-5
QMAX = 32767.0


class Queue:

    def __init__(self, eng, sem):
        self.eng, self.sem, self.n, self.seen = eng, sem, 0, {}

    def __call__(self, fn, *waits, sig=True):
        need = {}
        for w in flat(waits):
            if self.seen.get(id(w[0]), 0) < w[1]:
                self.seen[id(w[0])] = w[1]
                need[id(w[0])] = w
        for s, v in need.values():
            self.eng.wait_ge(s, v)
        ins = fn(self.eng)
        if not sig:
            return None
        self.n += 1
        ins.then_inc(self.sem, 1)
        return (self.sem, self.n)

    def wait(self, *waits):
        for s, v in flat(waits):
            if self.seen.get(id(s), 0) < v:
                self.seen[id(s)] = v
                self.eng.wait_ge(s, v)

    def last(self):
        return (self.sem, self.n)


def flat(ws):
    for w in ws:
        if w is None:
            continue
        if isinstance(w, list):
            yield from flat(w)
        else:
            yield w


def bc(ap, axis, n):
    shape = list(ap.shape)
    return ap.unsqueeze(axis).broadcast_to(shape[:axis] + [n] + shape[axis:])


class Stream:

    def __init__(self, sem):
        self.sem, self.n = sem, 0

    def token(self):
        return (self.sem, self.n) if self.n else None


def build(nc, a):
    ctx = ExitStack()
    with ctx:
        def sem(name):
            return ctx.enter_context(nc.semaphore(name))

        def dram(name, shape, dt):
            return nc.dram_tensor(name, shape, dt).ap()

        pe, act, dve, pool, sp = (Queue(g, sem(n)) for g, n in (
            (nc.tensor, "s_pe"), (nc.scalar, "s_act"), (nc.vector, "s_dve"), (nc.gpsimd, "s_pool"), (nc.sync, "s_sp")))
        streams = {}

        def dma(q, name, out, in_, *waits, **kw):
            if name not in streams:
                streams[name] = Stream(sem("d_" + name))
            st = streams[name]
            st.n += 16
            q(lambda e, st=st: e.dma_start(out, in_, **kw).then_inc(st.sem, 16), *waits, sig=False)
            return (st.sem, st.n)

        x1d = dram("x1d", (T, D), F32)
        x2d = dram("x2d", (T, D), F32)
        qd = dram("qd", (3, 3, 256, 256), BF16)
        kd = dram("kd", (3, 3, 256, 256), BF16)
        bufd = dram("bufd", (EC, D), F32)
        yd = dram("yd", (EC, D), F32)

        PS = ctx.enter_context(nc.psum_tensor("PS", [128, 8, 512], F32))
        bank_free = [None] * 8

        class Mem:

            count = 0

            def __init__(self):
                self.c = ExitStack()
                self.n = 0

            def __call__(self, name, shape, dt):
                Mem.count += 1
                return self.c.enter_context(nc.sbuf_tensor(f"{name}_{Mem.count}", shape, dt))

            def free(self):
                self.c.close()

        fix = Mem()
        ident = fix("ident", [128, 128], F32)
        identb = fix("identb", [128, 128], BF16)
        ones = fix("ones", [128, 128], F32)
        onesb = fix("onesb", [128, 128], BF16)
        triu = fix("triu", [128, 128], BF16)
        rev = fix("rev", [128, 2, 32], F32)
        gates = fix("gates", [128, 4], F32)
        tg = fix("tg", [128, 4], F32)
        bias_row = fix("bias_row", [128, 2, D], F32)
        tgb = fix("tgb", [128, 2, D], F32)
        mhalf = fix("mhalf", [128, 2], F32)
        sc = fix("sc", [128, 64], F32)
        wup = fix("wup", [128, 2, FF], F32)
        wgt = fix("wgt", [128, 2, FF], F32)
        wdn = fix("wdn", [128, 6, D], F32)

        t = [pool(lambda e, m=m, v=v: e.memset(m, v)) for m, v in (
            (ident[:, :], 0.0), (identb[:, :], 0.0), (ones[:, :], 1.0), (onesb[:, :], 1.0),
            (triu[:, :], 1.0), (mhalf[:, :], -0.5))]
        for m in (ident, identb):
            pool(lambda e, m=m: e.affine_select(out=m[:, :], in_=m[:, :], compare_op=ALU.not_equal, fill=1.0,
                                                base=0, pattern=[[-1, 128]], channel_multiplier=1), t)
        pool(lambda e: e.affine_select(out=triu[:, :], in_=triu[:, :], compare_op=ALU.is_ge, fill=0.0,
                                       base=0, pattern=[[1, 128]], channel_multiplier=-1), t)
        consts = pool(lambda e: e.iota(rev[:, :, :], pattern=[[0, 2], [-1, 32]], base=32, channel_multiplier=0,
                                       allow_small_or_imprecise_dtypes=True))
        g0 = dma(sp, "g", gates[:, 0:2], a["g_xattn"].rearrange("(o n) -> o n", o=1).broadcast_to([128, 2]))
        g0 = dma(sp, "g", gates[:, 2:4], a["g_ffn"].rearrange("(o n) -> o n", o=1).broadcast_to([128, 2]))
        g0 = dma(sp, "g", bias_row[:, 0, :], a["b0"].rearrange("(o n) -> o n", o=1).broadcast_to([128, D]))
        g0 = dma(sp, "g", bias_row[:, 1, :], a["b1"].rearrange("(o n) -> o n", o=1).broadcast_to([128, D]))
        t_tg = act(lambda e: e.activation(tg[:, :], gates[:, :], ACT.Tanh), g0)
        for i in range(2):
            t_tgb = pool(lambda e, i=i: e.tensor_scalar(tgb[:, i, :], bias_row[:, i, :], tg[:, i:i + 1], 0.0,
                                                        ALU.mult, ALU.add), t_tg, g0)

        def quantized_weights():
            m = Mem()
            w = m("w_nat", [128, 3, 1536], F32)
            q = m("w_q", [128, 1536], I16)
            s = m("w_s", [128, 3, 48], F32)
            r = m("w_r", [128, 3, 48], F32)
            ld = [dma(sp, "wq", w[:, i, :].rearrange("p (m n) -> p m n", m=k),
                      a[n].rearrange("(m p) n -> p m n", p=128))
                  for i, (n, k) in enumerate((("wup", 6), ("wgate", 6), ("wdown", 2)))]
            freed = []
            for i, (dst, kt) in enumerate(((wup, 2), (wgt, 2), (wdn, 6))):
                v = w[:, i, :].rearrange("p (b j) -> p b j", j=32)
                t = dve(lambda e, v=v, i=i: e.tensor_reduce(s[:, i, :], v, X, ALU.max, apply_absolute_value=True), ld)
                t = dve(lambda e, i=i: e.tensor_scalar(s[:, i, :], s[:, i, :], 1.0 / 7.0, 1e-12, ALU.mult, ALU.max), t)
                t = dve(lambda e, i=i: e.reciprocal(r[:, i, :], s[:, i, :]), t)
                t = dve(lambda e, v=v, i=i: e.tensor_tensor(v, v, bc(r[:, i, :], 2, 32), ALU.mult), t)
                t = dve(lambda e, v=v: e.tensor_scalar(q[:, :], w[:, i, :] if False else v.rearrange("p b j -> p (b j)"),
                                                       7.0, -8.0, ALU.min, ALU.max), t)
                t = dve(lambda e, v=v, i=i: e.tensor_tensor(v, q[:, :].rearrange("p (b j) -> p b j", j=32),
                                                            bc(s[:, i, :], 2, 32), ALU.mult), t)
                cols = 1536 // (kt * 128)
                for k in range(kt):
                    for mt in range(0, cols, 2):
                        n = min(2, cols - mt)
                        bk = 6 + (k * cols + mt) // 2 % 2
                        for j in range(n):
                            src = w[:, i, (mt + j) * kt * 128 + k * 128:(mt + j) * kt * 128 + (k + 1) * 128]
                            p = pe(lambda e, src=src, bk=bk, j=j: e.transpose(
                                PS[:, bk, 128 * j:128 * j + 128], src, ident[:, :]), t, consts, bank_free[bk])
                        bank_free[bk] = act(lambda e, dst=dst, bk=bk, k=k, mt=mt, n=n: e.activation(
                            dst[:, k, mt * 128:(mt + n) * 128], PS[:, bk, 0:128 * n], ACT.Copy), p)
                        freed.append(bank_free[bk])
            m.free()
            return [freed[-1], dve.last(), pe.last()]

        t_wq = quantized_weights()

        def all_done():
            t = [q.last() for q in (pe, act, dve, pool) if q.n] + [s.token() for s in streams.values()]
            for q in (pe, act, dve, pool, sp):
                q.wait(t)
            return t

        scn = [0]

        def scalar_col(n=1):
            c = scn[0]
            scn[0] += n
            return c

        def global_scale(col, ncols, src, *waits):
            c = scalar_col(3)
            t = dve(lambda e: e.tensor_reduce(sc[:, c:c + 1], src, X, ALU.max), *waits)
            p = pe(lambda e: e.transpose(PS[0:1, 7, 0:128], sc[:, c:c + 1], ident[:, :]), t, consts, bank_free[7])
            t = dve(lambda e: e.tensor_reduce(sc[0:1, c + 1:c + 2], PS[0:1, 7, 0:128], X, ALU.max), p)
            p = pe(lambda e: e.matmul(PS[:, 7, 128:129], ones[0:1, :], sc[0:1, c + 1:c + 2], start=True, stop=True), t)
            t = dve(lambda e: e.tensor_scalar(sc[:, c:c + 1], PS[:, 7, 128:129], 1.0 / QMAX, 1e-12,
                                              ALU.mult, ALU.max), p)
            bank_free[7] = t
            t = dve(lambda e: e.reciprocal(sc[:, c + 2:c + 3], sc[:, c:c + 1]), t)
            return sc[:, c:c + 1], sc[:, c + 2:c + 3], t

        def layer_norm(tag, x, out, st, t_x, nb, extra=None, free=None):
            for i in range(2):
                t = dve(lambda e, i=i: e.bn_stats(st[:, 16 + 6 * i:22 + 6 * i], x[:, i, :]), t_x, free)
            for i in range(2):
                t = dve(lambda e, i=i: e.bn_aggr(st[:, 2 * i:2 * i + 2], st[:, 16 + 6 * i:22 + 6 * i]), t)
            mv = st[:, 0:4].rearrange("p (t k) -> p t k", k=2)
            t1 = dve(lambda e: e.tensor_scalar(st[:, 4:6], mv[:, :, 0], -1.0, None, ALU.mult), t)
            t2 = dve(lambda e: e.tensor_scalar(st[:, 6:8], mv[:, :, 1], EPS, None, ALU.add), t)
            t = pool(lambda e: e.tensor_tensor(st[:, 8:10], st[:, 6:8], mhalf[:, :], ALU.pow), t2, consts)
            if extra is not None:
                t = pool(lambda e: e.tensor_tensor(st[:, 8:10], st[:, 8:10], extra[0], ALU.mult), t, extra[1])
            for i in range(2):
                t = pool(lambda e, i=i: e.tensor_scalar(out[:, i, :], x[:, i, :], st[:, 4 + i:5 + i],
                                                        st[:, 8 + i:9 + i], ALU.add, ALU.mult), t, t1, free)
            return t

        def attention(L, m, xin, t_xin, epilogue, keep):
            XB = [m(f"XB{i}", [128, 2, D], F32) for i in range(5)]
            XN = m("XN", [128, 2, D], F32)
            ST = [m(f"ST{i}", [128, 32], F32) for i in range(2)]
            XT = m("XT", [128, 2, 256], F32)
            CT = [m(f"CT{i}", [128, 2, 256], F32) for i in range(2)]
            W = {n: m("W" + n, [128, 2, D], F32) for n in "qkvo"}
            QF = m("QF", [128, 512], F32)
            R1 = m("R1", [128, 512], F32)
            PP = [m(f"PP{i}", [128, 2, 3, 256], BF16) for i in range(2)]
            QS = [m(f"QS{i}", [100, H, 256], BF16) for i in range(3)]
            KS = [m(f"KS{i}", [100, H, 256], BF16) for i in range(3)]
            V = [m(f"V{i}", [128, 2, H, 32], F32) for i in range(3)]
            P = [m(f"P{i}", [128, 2, 256], F32) for i in range(4)]
            OT = [m(f"OT{i}", [128, 4, 256], F32) for i in range(2)]
            ON = m("ON", [128, 2, 256], F32)
            ONT = m("ONT", [128, 2, 256], F32)
            RD = m("RD", [128, 2, H], F32)
            NM = [m(f"NM{i}", [128, 2, H], F32) for i in range(2)]
            NH = m("NH", [128, 2, 2, 8], BF16)
            NR = m("NR", [128, 2, 8], F32)
            NP = m("NP", [128, 2, 3, 8], F32)
            NT = [m(f"NT{i}", [24, 256], BF16) for i in range(2)]
            if L == 0:
                MQ = [m(f"MQ{i}", [128, 2, 256], U8) for i in range(2)]
                MT = [m(f"MT{i}", [128, 2, 256], U8) for i in range(2)]
                AV = [m(f"AV{i}", [128, 2], F32) for i in range(2)]
                NQ = [m(f"NQ{i}", [128, 2, 256], BF16) for i in range(3)]
                NK = [m(f"NK{i}", [128, 2, 256], BF16) for i in range(3)]
            for n in "qkvo":
                t_w = dma(sp, f"w{L}", W[n][:, :, :], a[f"w{n}{L}"].rearrange("(k p) n -> p k n", p=128), keep)
            init = []
            for i in range(3):
                init.append(dve(lambda e, i=i: e.memset(QS[i][96:100, :, :], 1.0), keep))
                init.append(dve(lambda e, i=i: e.memset(KS[i][96:100, :, :], 1.0), keep))
                t = dve(lambda e, i=i: e.memset(V[i][:, :, :, :], 0.0), keep)
                init.append(dve(lambda e, i=i: e.memset(V[i][:, :, :, 16:17], 1.0), t))
            for i in range(3):
                init.append(dve(lambda e, i=i: e.memset(KS[i][96:97, :, :], 0.0), init[-1]))
            init = [init[-1]]
            misc = [0]
            tok = {}

            def bank():
                misc[0] ^= 1
                return 6 + misc[0]

            def g(k, b):
                return tok.get((k, b))

            def put(k, b, v):
                tok[(k, b)] = v

            def load(b):
                i = b % 5
                put("x", b, dma(sp, f"x{L}{i}", XB[i][:, :, :], xin[b * S:(b + 1) * S, :].rearrange(
                    "(t p) d -> p t d", p=128), keep, t_xin(b), g("xfree", b - 5)))
                j = b % 2
                put("ct", b, dma(sp, f"c{L}{j}", CT[j][:, :, :], a["ctxT"][:, b * S:(b + 1) * S].rearrange(
                    "(k p) n -> p k n", p=128), keep, g("ctfree", b - 2)))
                if L == 0:
                    put("m", b, [dma(sp, f"m{j}", MQ[j][:, :, :], a["mq"][b].rearrange("(t p) n -> p t n", p=128),
                                     keep, g("mfree", b - 2)),
                                 dma(sp, f"m{j}", MT[j][:, :, :], a["mt"][b].rearrange("(t p) n -> p t n", p=128),
                                     keep, g("mfree", b - 2))])

            def split(which, b, bk, p, scale):
                pp = PP[0 if which == "q" else 1]
                ppv = pp[:, :, :, :]
                st = (QS if which == "q" else KS)[b % 3]
                dd = (qd if which == "q" else kd)[b % 3]
                bankv = PS[:, bk, :]
                fr = g("split", 0)
                t1 = act(lambda e: e.activation(QF[:, :], bankv, ACT.Copy, scale=scale), p, fr)
                th = act(lambda e: e.activation(ppv[:, :, 0, :], bankv.rearrange("p (m n) -> p m n", m=2), ACT.Copy,
                                                scale=scale), g(which + "sent", 0))
                bank_free[bk] = th
                qf = QF[:, :].rearrange("p (m n) -> p m n", m=2)
                r1 = R1[:, :].rearrange("p (m n) -> p m n", m=2)
                t = pool(lambda e: e.tensor_tensor(r1, qf, ppv[:, :, 0, :], ALU.subtract), t1, th)
                t = dve(lambda e: e.tensor_copy(ppv[:, :, 1, :], r1), t)
                t = pool(lambda e: e.tensor_tensor(ppv[:, :, 2, :], r1, ppv[:, :, 1, :], ALU.subtract), t)
                put("split", 0, t)
                sent = []
                for part in range(3):
                    sent = dma(sp, f"{which}w", dd[part].rearrange("(m p) n -> p m n", p=128), ppv[:, :, part, :],
                               t, g(which + "st", b - 3))
                put(which + "sent", 0, sent)
                free = [g("c", b - 3), g("bdone", b - 3), init[0]]
                flatd = dd.rearrange("s (r h) n -> s r (h n)", h=H)
                if which == "q":
                    for part in range(3):
                        tt = dma(sp, f"{which}s{b % 3}", st[16 * part:16 * part + 16, :, :].rearrange(
                            "p h n -> p (h n)"), flatd[part], sent, free)
                    for part in range(2):
                        tt = dma(sp, f"{which}s{b % 3}", st[48 + 16 * part:64 + 16 * part, :, :].rearrange(
                            "p h n -> p (h n)"), flatd[part])
                    tt = dma(sp, f"{which}s{b % 3}", st[80:96, :, :].rearrange("p h n -> p (h n)"), flatd[0])
                else:
                    for s_, part in enumerate((0, 0, 0, 1, 1, 2)):
                        tt = dma(sp, f"{which}s{b % 3}", st[16 * s_:16 * s_ + 16, :, :].rearrange(
                            "p h n -> p (h n)"), flatd[part], sent, free)
                put(which + "st", b, tt)

            def project(w, src, bk, t):
                for mt in range(2):
                    for k in range(2):
                        p = pe(lambda e, mt=mt, k=k: e.matmul(
                            PS[:, bk, 256 * mt:256 * mt + 256], W[w][:, k, 128 * mt:128 * mt + 128], src[:, k, :],
                            start=(k == 0), stop=(k == 1)), t, t_w, bank_free[bk], sig=(mt + k == 2))
                return p

            def stA(b):
                j = b % 2
                ct = CT[j]
                bk = bank()
                p = project("k", ct, bk, g("ct", b))
                split("k", b, bk, p, 1.0)
                yield
                ex = None
                if L == 0:
                    t = dve(lambda e: e.tensor_reduce(AV[j][:, :], MQ[j][:, :, :], X, ALU.max), g("m", b), g("xn", b - 2))
                    ex = (AV[j][:, :], t)
                    pool(lambda e: e.tensor_scalar(NQ[b % 3][:, :, :], MQ[j][:, :, :], -1.0, -NEG, ALU.add, ALU.mult),
                         g("m", b), g("bdone", b - 3))
                    tn = pool(lambda e: e.tensor_scalar(NK[b % 3][:, :, :], MT[j][:, :, :], -1.0, -NEG, ALU.add,
                                                        ALU.mult), g("c", b - 3))
                    put("mfree", b, [tn, t])
                    put("pen", b, tn)
                yield
                t = layer_norm("a", XB[b % 5], XN, ST[j], g("x", b), b, ex, [g("xtr", b - 1), g("xn", b - 2)])
                put("xn", b, t)
                put("xb", b, pool(lambda e: e.tensor_tensor(
                    XB[b % 5][:, :, :], XB[b % 5][:, :, :], bc(tgb[:, L, :], 1, 2), ALU.add),
                    t, t_tgb))
                yield
                bk = bank()
                for kt in range(2):
                    for tt in range(2):
                        p = pe(lambda e, kt=kt, tt=tt: e.transpose(
                            PS[:, bk, 256 * kt + 128 * tt:256 * kt + 128 * tt + 128],
                            XN[:, tt, 128 * kt:128 * kt + 128], ident[:, :]), t, consts, bank_free[bk], sig=(kt + tt == 2))
                put("xtr", b, p)
                bank_free[bk] = t = act(lambda e: e.activation(
                    XT[:, :, :], PS[:, bk, :].rearrange("p (k n) -> p k n", k=2), ACT.Copy), p, g("qp", b - 1))
                yield
                yield
                bk = bank()
                p = project("q", XT, bk, t)
                put("qp", b, p)
                split("q", b, bk, p, 0.25)
                yield
                yield
                bk = bank()
                for tt in range(2):
                    for k in range(2):
                        p = pe(lambda e, tt=tt, k=k: e.matmul(
                            PS[:, bk, 256 * tt:256 * tt + 256], ct[:, k, 128 * tt:128 * tt + 128], W["v"][:, k, :],
                            start=(k == 0), stop=(k == 1)), g("ct", b), bank_free[bk], sig=(tt + k == 2))
                put("ctfree", b, p)
                bank_free[bk] = act(lambda e: e.activation(
                    V[b % 3][:, :, :, 0:16], PS[:, bk, :].rearrange("p (t h r) -> p t h r", t=2, h=H), ACT.Copy),
                    p, g("av", b - 3), init)
                put("v", b, bank_free[bk])
                yield

            def stB(b):
                Q, K = QS[b % 3], KS[b % 3]
                nm = NM[b % 2]
                for h in range(H):
                    bk = 3 + h % 2
                    for qt in range(2):
                        o = PS[:, bk, 256 * qt:256 * qt + 256]
                        p = pe(lambda e, o=o, h=h, qt=qt: e.matmul(
                            o, Q[0:97, h, 128 * qt:128 * qt + 128], K[0:97, h, :], start=True, stop=(L == 1)),
                            g("qst", b), g("kst", b), bank_free[bk], sig=(L == 1 and qt == 1))
                        if L == 0:
                            p = pe(lambda e, o=o, qt=qt: e.matmul(o, identb[:, :], NQ[b % 3][:, qt, :], start=False,
                                                                  stop=True), g("pen", b), sig=(qt == 1))
                    bank_free[bk] = dve(lambda e, h=h, bk=bk: e.tensor_reduce(
                        nm[:, :, h], PS[:, bk, :].rearrange("p (t n) -> p t n", t=2), X, ALU.max, negate=True),
                        p, g("nm", b - 2))
                    if h % 8 == 7:
                        hh = h // 8
                        v = nm[:, :, 8 * hh:8 * hh + 8]
                        t = dve(lambda e, v=v: e.tensor_copy(NH[:, 0, :, :], v), bank_free[bk], g("nfree", 0))
                        t0 = pool(lambda e: e.tensor_copy(NP[:, :, 0, :], NH[:, 0, :, :]), t, g("ntr", 0))
                        t = dve(lambda e, v=v: e.tensor_tensor(NR[:, :, :], v, NH[:, 0, :, :], ALU.subtract), t)
                        t = dve(lambda e: e.tensor_copy(NH[:, 1, :, :], NR[:, :, :]), t)
                        t1 = pool(lambda e: e.tensor_copy(NP[:, :, 1, :], NH[:, 1, :, :]), t)
                        t = dve(lambda e: e.tensor_tensor(NP[:, :, 2, :], NR[:, :, :], NH[:, 1, :, :], ALU.subtract),
                                t, g("ntr", 0))
                        put("nfree", 0, t1)
                        if hh == 1:
                            put("nm", b, t)
                        yield
                        mb = bank()
                        for qt in range(2):
                            p = pe(lambda e, qt=qt: e.transpose(
                                PS[0:24, mb, 128 * qt:128 * qt + 128],
                                NP[:, qt, :, :].rearrange("p a h -> p (a h)"), ident[:, :]),
                                t, t1, consts, bank_free[mb], sig=(qt == 1))
                        put("ntr", 0, p)
                        nt = NT[hh]
                        bank_free[mb] = t = act(lambda e, nt=nt: e.activation(nt[:, :], PS[0:24, mb, 0:256], ACT.Copy),
                                                p, g("nsent%d" % hh, 0))
                        for part in range(3):
                            s = dma(sp, f"n{hh}{b % 3}", Q[97 + part:98 + part, 8 * hh:8 * hh + 8, :],
                                    nt[8 * part:8 * part + 8, :], t, g("c", b - 3), init)
                        put("nsent%d" % hh, 0, s)
                        put("nst%d" % hh, b, s)
                    else:
                        yield

            def av(b, h):
                gi, i = h // 4, h % 4
                for kt in range(2):
                    p = pe(lambda e, kt=kt: e.matmul(
                        PS[32 * i:32 * i + 32, 5, 256 * (gi % 2):256 * (gi % 2) + 256],
                        V[b % 3][:, kt, h, :], P[h % 4][:, kt, :], start=(kt == 0), stop=(kt == 1)),
                        g("p", (b, h)), g("v", b), bank_free[5] if h % 8 == 0 else None, sig=(kt == 1))
                put("avp", h % 4, p)
                if h == H - 1:
                    put("av", b, p)
                if h % 8 == 7:
                    hh = h // 8
                    bank_free[5] = act(lambda e: e.activation(
                        OT[b % 2][:, 2 * hh:2 * hh + 2, :], PS[:, 5, :].rearrange("p (g n) -> p g n", g=2), ACT.Copy),
                        p, g("otr", b - 2))
                    put("ot", b, bank_free[5])

            def stC(b):
                Q, K = QS[b % 3], KS[b % 3]
                for h in range(H):
                    bk = h % 3
                    for kt in range(2):
                        o = PS[:, bk, 256 * kt:256 * kt + 256]
                        p = pe(lambda e, o=o, h=h, kt=kt: e.matmul(
                            o, K[0:100, h, 128 * kt:128 * kt + 128], Q[0:100, h, :], start=True, stop=(L == 1)),
                            g("nst%d" % (h // 8), b), bank_free[bk], sig=(L == 1 and kt == 1))
                        if L == 0:
                            p = pe(lambda e, o=o, kt=kt: e.matmul(o, identb[:, :], NK[b % 3][:, kt, :], start=False,
                                                                  stop=True), g("pen", b), sig=(kt == 1))
                    if h == H - 1:
                        put("c", b, p)
                    bank_free[bk] = act(lambda e, h=h, bk=bk: e.activation(
                        P[h % 4][:, :, :], PS[:, bk, :].rearrange("p (k n) -> p k n", k=2), ACT.Exp), p,
                        g("avp", h % 4))
                    put("p", (b, h), bank_free[bk])
                    if h >= 2:
                        av(b, h - 2)
                    yield

            def stD(b):
                av(b, H - 2)
                yield
                av(b, H - 1)
                yield
                for qt in range(2):
                    bk = bank()
                    for gi in range(4):
                        p = pe(lambda e, gi=gi, qt=qt, bk=bk: e.transpose(
                            PS[:, bk, 128 * gi:128 * gi + 128], OT[b % 2][:, gi, 128 * qt:128 * qt + 128],
                            ident[:, :]), g("ot", b), bank_free[bk], sig=(gi == 3))
                    pv = PS[:, bk, :].rearrange("p (h r) -> p h r", r=32)
                    t = dve(lambda e, qt=qt, pv=pv: e.reciprocal(RD[:, qt, :], pv[:, :, 16]), p)
                    bank_free[bk] = t = dve(lambda e, qt=qt, pv=pv: e.tensor_tensor(
                        ON[:, qt, :].rearrange("p (h r) -> p h r", r=16), pv[:, :, 0:16],
                        bc(RD[:, qt, :], 2, 16), ALU.mult), t, g("ontr", b - 1))
                    if qt == 1:
                        put("otr", b, p)
                    yield
                bk = bank()
                for kt in range(2):
                    for qt in range(2):
                        p = pe(lambda e, kt=kt, qt=qt: e.transpose(
                            PS[:, bk, 256 * kt + 128 * qt:256 * kt + 128 * qt + 128],
                            ON[:, qt, 128 * kt:128 * kt + 128], ident[:, :]), t, bank_free[bk], sig=(kt + qt == 2))
                put("ontr", b, p)
                bank_free[bk] = t = act(lambda e: e.activation(
                    ONT[:, :, :], PS[:, bk, :].rearrange("p (k n) -> p k n", k=2), ACT.Copy), p, g("op", b - 1))
                yield
                bk = bank()
                for qt in range(2):
                    for k in range(2):
                        p = pe(lambda e, qt=qt, k=k: e.matmul(
                            PS[:, bk, 256 * qt:256 * qt + 256], ONT[:, k, 128 * qt:128 * qt + 128],
                            W["o"][:, k, :], start=(k == 0), stop=(k == 1)), t, bank_free[bk], sig=(qt + k == 2))
                put("op", b, p)
                xb = XB[b % 5]
                bank_free[bk] = t = dve(lambda e: e.scalar_tensor_tensor(
                    xb[:, :, :], PS[:, bk, :].rearrange("p (t n) -> p t n", t=2), tg[:, L:L + 1], xb[:, :, :],
                    ALU.mult, ALU.add), p, g("xb", b), t_tg)
                yield
                yield from epilogue(b, xb, t, bank, ST[b % 2], g, put)

            load(0)
            for s in range(-2, NB + 1):
                if s + 3 < NB:
                    load(s + 3)
                gens = []
                if 0 <= s < NB:
                    gens.append(stC(s))
                if 0 <= s + 1 < NB:
                    gens.append(stB(s + 1))
                if 0 <= s + 2 < NB:
                    gens.append(stA(s + 2))
                if 0 <= s - 1:
                    gens.append(stD(s - 1))
                while gens:
                    gens = [x for x in gens if next(x, "end") != "end"]
            return all_done()

        top = Mem()
        XNT = top("XNT", [128, 2, T], F32)
        AM = top("AM", [128, 96], F32)
        m = Mem()
        XM = m("XM", [128, 2, D], F32)
        ST0 = m("ST0", [128, 32], F32)

        def epi0(b, xb, t, bank, st, g, put):
            put("x1", b, dma(sp, f"x1{b % 4}", x1d[b * S:(b + 1) * S, :].rearrange("(t p) d -> p t d", p=128),
                             xb[:, :, :], t))
            t = layer_norm("e", xb, XM, ST0, t, b, None, [g("xmtr", b - 1), g("xm", b - 1)])
            put("xm", b, t)
            put("xfree", b, [t, g("x1", b)])
            yield
            bk = bank()
            for kt in range(2):
                for tt in range(2):
                    p = pe(lambda e, kt=kt, tt=tt: e.transpose(
                        PS[:, bk, 256 * kt + 128 * tt:256 * kt + 128 * tt + 128],
                        XM[:, tt, 128 * kt:128 * kt + 128], ident[:, :]), t, bank_free[bk], sig=(kt + tt == 2))
            put("xmtr", b, p)
            dst = XNT[:, :, b * S:(b + 1) * S]
            bank_free[bk] = t = act(lambda e: e.activation(
                dst, PS[:, bk, :].rearrange("p (k n) -> p k n", k=2), ACT.Copy), p)
            t_am[0] = dve(lambda e: e.tensor_reduce(AM[:, b:b + 1], dst, mybir.AxisListType.XY, ALU.max,
                                                    apply_absolute_value=True), t)
            x1_t[b] = g("x1", b)
            yield

        t_am, x1_t = [None], {}
        done0 = attention(0, m, a["x"], lambda b: None, epi0, t_wq)
        m.free()

        m = Mem()
        G = m("G", [128, 6, T], F32)
        UQ = m("UQ", [128, 6, T], I16)
        Gf = G[:, :, :].rearrange("p m n -> p (m n)")
        UQf = UQ[:, :, :].rearrange("p m n -> p (m n)")
        s1, i1, t = global_scale(0, 16, AM[:, 0:16], t_am[0])
        tq = {}
        for n in range(8):
            v = XNT[:, :, 512 * n:512 * n + 512]
            q = UQ[:, 0:2, 512 * n:512 * n + 512]
            t2 = dve(lambda e, v=v, q=q: e.tensor_scalar(q, v, i1, QMAX, ALU.mult, ALU.min), t, done0)
            tq[n] = act(lambda e, v=v, q=q: e.activation(v, q, ACT.Copy, scale=s1), t2)

        def ff_in(w, wait, col):
            out = None
            for n in range(8):
                for mt in range(6):
                    bk = (n * 6 + mt) % 7
                    for k in range(2):
                        p = pe(lambda e, k=k, mt=mt, n=n, bk=bk: e.matmul(
                            PS[:, bk, :], w[:, k, 128 * mt:128 * mt + 128], XNT[:, k, 512 * n:512 * n + 512],
                            start=(k == 0), stop=(k == 1)), tq[n], bank_free[bk], sig=(k == 1))
                    dst = G[:, mt, 512 * n:512 * n + 512]
                    bank_free[bk] = t = act(lambda e, dst=dst, bk=bk: e.activation(dst, PS[:, bk, :], ACT.Copy), p,
                                            wait(mt, n))
                    c = n * 6 + mt
                    out = dve(lambda e, dst=dst, c=c: e.tensor_reduce(
                        AM[:, col + c:col + c + 1], dst, X, ALU.max, apply_absolute_value=True), t)
            return out

        t = ff_in(wup, lambda mt, n: None, 48 * 0)
        s2, i2, t = global_scale(0, 48, AM[:, 0:48], t)
        tu = {}
        for n in range(8):
            v, q = G[:, :, 512 * n:512 * n + 512], UQ[:, :, 512 * n:512 * n + 512]
            tu[n] = dve(lambda e, v=v, q=q: e.tensor_scalar(q, v, i2, QMAX, ALU.mult, ALU.min), t, tq[7])
        t = ff_in(wgt, lambda mt, n: tu[n], 48)
        s3, i3, t = global_scale(0, 48, AM[:, 48:96], t)
        top2 = Mem()
        NCH = 24
        CW = 6 * T // NCH
        XNf = XNT[:, :, :].rearrange("p k n -> p (k n)")
        GQ = [XNf[:, 2048 * i:2048 * i + CW // 2].bitcast(I16) for i in range(2)]
        SG = [XNf[:, 4096 + 1024 * i:4096 + 1024 * i + CW] for i in range(2)]
        SQ = [XNf[:, 6144 + 1024 * i:6144 + 1024 * i + CW // 2].bitcast(U16) for i in range(2)]
        prev = {}
        pend = []

        def gate_tail(c):
            j = c % 2
            v = Gf[:, CW * c:CW * c + CW]
            t = dve(lambda e, j=j: e.tensor_scalar(SQ[j], SG[j], 65536.0, 65535.0, ALU.mult, ALU.min), prev["sig", c])
            t = dve(lambda e, j=j, v=v: e.scalar_tensor_tensor(v, GQ[j], s3, SQ[j], ALU.mult, ALU.mult), t)
            prev["gq", c] = t
            return dve(lambda e, v=v, c=c: e.tensor_reduce(AM[:, c:c + 1], v, X, ALU.max, apply_absolute_value=True), t)

        t0 = t
        for c in range(NCH):
            j = c % 2
            v = Gf[:, CW * c:CW * c + CW]
            t = dve(lambda e, v=v, j=j: e.tensor_scalar(GQ[j], v, i3, QMAX, ALU.mult, ALU.min), t0, prev.get(("gq", c - 2)),
                    pe.last())
            prev["sig", c] = act(lambda e, j=j: e.activation(SG[j], GQ[j], ACT.Sigmoid, scale=s3), t,
                                 prev.get(("gq", c - 2)))
            if c:
                t = gate_tail(c - 1)
        t = gate_tail(NCH - 1)
        s4, i4, t = global_scale(0, NCH, AM[:, 0:NCH], t)
        for c in range(NCH):
            j = c % 2
            v, u = Gf[:, CW * c:CW * c + CW], UQf[:, CW * c:CW * c + CW]
            t1 = dve(lambda e, v=v, j=j: e.tensor_scalar(GQ[j], v, i4, QMAX, ALU.mult, ALU.min), t)
            t1 = dve(lambda e, v=v, u=u, j=j: e.tensor_tensor(v, GQ[j], u, ALU.mult), t1)
            t2 = dve(lambda e, v=v, c=c: e.tensor_reduce(AM[:, 32 + c:33 + c], v, X, ALU.max,
                                                         apply_absolute_value=True), t1)
        s5, i5, t = global_scale(0, NCH, AM[:, 32:32 + NCH], t2)
        c = scalar_col(2)
        fs = sc[:, c:c + 1]
        t5 = dve(lambda e: e.tensor_scalar(fs, s5, s4, s2, ALU.mult, ALU.mult), t)
        t5 = dve(lambda e: e.tensor_scalar(fs, fs, tg[:, 2:3], 1.0 / 65536.0, ALU.mult, ALU.mult), t5)
        XD = [m(f"XD{i}", [128, 2, D], F32) for i in range(2)]
        x2_t = {}
        stt = {}
        for b in range(NB):
            v = G[:, :, 256 * b:256 * b + 256]
            q = UQ[:, :, 256 * b:256 * b + 256]
            t1 = dve(lambda e, v=v, q=q: e.tensor_scalar(q, v, i5, QMAX, ALU.mult, ALU.min), t)
            t1 = act(lambda e, v=v, q=q: e.activation(v, q, ACT.Copy), t1)
            ld = dma(sp, f"xd{b % 2}", XD[b % 2][:, :, :], x1d[b * S:(b + 1) * S, :].rearrange(
                "(t p) d -> p t d", p=128), x1_t[b], stt.get(b - 2), done0)
            bk = b % 7
            for tt in range(2):
                for k in range(6):
                    p = pe(lambda e, b=b, tt=tt, k=k, bk=bk: e.matmul(
                        PS[:, bk, 256 * tt:256 * tt + 256], G[:, k, 256 * b + 128 * tt:256 * b + 128 * tt + 128],
                        wdn[:, k, :], start=(k == 0), stop=(k == 5)), t1, bank_free[bk], sig=(tt == 1 and k == 5))
            bank_free[bk] = t2 = dve(lambda e, b=b, bk=bk: e.scalar_tensor_tensor(
                XD[b % 2][:, :, :], PS[:, bk, :].rearrange("p (t n) -> p t n", t=2), fs, XD[b % 2][:, :, :],
                ALU.mult, ALU.add), p, ld, t5)
            stt[b] = x2_t[b] = dma(sp, f"x2{b % 4}", x2d[b * S:(b + 1) * S, :].rearrange("(t p) d -> p t d", p=128),
                                   XD[b % 2][:, :, :], t2)
        done1 = all_done()
        m.free()
        top.free()

        top = Mem()
        BASE = top("BASE", [128, 32, D], F32)
        GG = top("GG", [128, 32], F32)
        SLG = top("SLG", [128, 32], I32)
        SLS = top("SLS", [128, 32], I32)
        m = Mem()
        XM = m("XM1", [128, 2, D], F32)
        ST0 = m("ST1", [128, 32], F32)
        XMT = m("XMT", [128, 2, 256], F32)
        WR = m("WR", [128, 2, E], F32)
        LG = m("LG", [128, 2, E], F32)
        EX = m("EX", [128, 2, E], F32)
        OHF = m("OHF", [128, 2, E], F32)
        OHB = m("OHB", [128, 2, E], BF16)
        CN = m("CN", [128, 33, E], BF16)
        RS = m("RS", [128, 16], F32)
        ZB = m("ZB", [128, D], F32)
        t_z = dve(lambda e: e.memset(ZB[:, :], 0.0), done1)
        for i in range(EC // 128 // 8):
            t_zd = dma(sp, "zero", bufd[1024 * i:1024 * i + 1024, :].rearrange("(t p) d -> p t d", p=128),
                       bc(ZB[:, :], 1, 8), t_z)
        t_c = dve(lambda e: e.memset(CN[:, 0, :], 0.0), done1)
        t_wr = dma(sp, "wr", WR[:, :, :], a["wr"].rearrange("(k p) n -> p k n", p=128), done1)
        cn_t = [t_c]
        sc_t = {}

        def epi1(b, xb, t, bank, st, g, put):
            t = layer_norm("e", xb, XM, ST0, t, b, None, [g("xmtr", b - 1), g("xm", b - 1), sc_t.get(b - 1)])
            put("xm", b, t)
            tb = dve(lambda e: e.scalar_tensor_tensor(BASE[:, 2 * b:2 * b + 2, :], XM[:, :, :], tg[:, 3:4],
                                                      xb[:, :, :], ALU.mult, ALU.add), t, done1)
            put("xfree", b, [t, tb])
            t_xm = t
            yield
            bk = bank()
            for kt in range(2):
                for tt in range(2):
                    p = pe(lambda e, kt=kt, tt=tt: e.transpose(
                        PS[:, bk, 256 * kt + 128 * tt:256 * kt + 128 * tt + 128],
                        XM[:, tt, 128 * kt:128 * kt + 128], ident[:, :]), t, bank_free[bk], sig=(kt + tt == 2))
            put("xmtr", b, [p, tb])
            bank_free[bk] = t = act(lambda e: e.activation(
                XMT[:, :, :], PS[:, bk, :].rearrange("p (k n) -> p k n", k=2), ACT.Copy), p, g("rt", b - 1))
            yield
            bk = bank()
            for tt in range(2):
                for kt in range(2):
                    p = pe(lambda e, kt=kt, tt=tt: e.matmul(
                        PS[:, bk, 32 * tt:32 * tt + 32], XMT[:, kt, 128 * tt:128 * tt + 128], WR[:, kt, :],
                        start=(kt == 0), stop=(kt == 1)), t, t_wr, bank_free[bk], sig=(kt + tt == 2))
            put("rt", b, p)
            bank_free[bk] = t = dve(lambda e: e.tensor_copy(
                LG[:, :, :], PS[:, bk, 0:64].rearrange("p (t n) -> p t n", t=2)), p)
            t = dve(lambda e: e.tensor_reduce(RS[:, 0:2], LG[:, :, :], X, ALU.max), t)
            t = dve(lambda e: e.tensor_scalar(RS[:, 2:4], RS[:, 0:2], -1.0, None, ALU.mult), t)
            for i in range(2):
                te = act(lambda e, i=i: e.activation(EX[:, i, :], LG[:, i, :], ACT.Exp, bias=RS[:, 2 + i:3 + i],
                                                     accum_out=RS[:, 4 + i:5 + i]), t)
            t = dve(lambda e: e.tensor_tensor(OHF[:, :, :], LG[:, :, :], bc(RS[:, 0:2], 2, E),
                                              ALU.is_equal), t)
            t = dve(lambda e: e.tensor_tensor(OHF[:, :, :], OHF[:, :, :], rev[:, :, :], ALU.mult), t)
            t = dve(lambda e: e.tensor_reduce(RS[:, 6:8], OHF[:, :, :], X, ALU.max), t)
            t = dve(lambda e: e.tensor_tensor(OHB[:, :, :], rev[:, :, :], bc(RS[:, 6:8], 2, E),
                                              ALU.is_equal), t, g("pos", b - 1))
            t_oh = t
            for i in range(2):
                n = 2 * b + i
                cn_t[0] = dve(lambda e, n=n, i=i: e.tensor_tensor(CN[:, n + 1, :], CN[:, n, :], OHB[:, i, :], ALU.add),
                              t_oh, cn_t[0])
            t_r = dve(lambda e: e.reciprocal(RS[:, 8:10], RS[:, 4:6]), te)
            yield
            bk = bank()
            for i in range(2):
                o = PS[:, bk, 32 * i:32 * i + 32]
                pe(lambda e, o=o, i=i: e.matmul(o, triu[:, :], OHB[:, i, :], start=True, stop=False),
                   t_oh, cn_t[0], bank_free[bk], sig=False)
                p = pe(lambda e, o=o, i=i: e.matmul(o, onesb[:, :], CN[:, 2 * b + i, :], start=False, stop=True))
            put("pos", b, p)
            bank_free[bk] = t = dve(lambda e: e.tensor_tensor(
                OHF[:, :, :], PS[:, bk, 0:64].rearrange("p (t n) -> p t n", t=2), OHB[:, :, :], ALU.mult), p)
            t = dve(lambda e: e.tensor_reduce(RS[:, 10:12], OHF[:, :, :], X, ALU.add), t)
            t = dve(lambda e: e.tensor_scalar(RS[:, 12:14], RS[:, 6:8], -float(C), float(C * E - 1), ALU.mult, ALU.add), t)
            t = dve(lambda e: e.tensor_tensor(RS[:, 12:14], RS[:, 12:14], RS[:, 10:12], ALU.add), t)
            t = dve(lambda e: e.tensor_scalar(RS[:, 10:12], RS[:, 10:12], float(C), None, ALU.is_le), t)
            dve(lambda e: e.tensor_tensor(GG[:, 2 * b:2 * b + 2], RS[:, 10:12], RS[:, 8:10], ALU.mult), t, t_r)
            t = dve(lambda e: e.tensor_tensor(RS[:, 12:14], RS[:, 12:14], RS[:, 10:12], ALU.mult), t)
            t = dve(lambda e: e.tensor_copy(SLG[:, 2 * b:2 * b + 2], RS[:, 12:14]), t)
            t1 = dve(lambda e: e.tensor_scalar(RS[:, 10:12], RS[:, 10:12], -1.0e6, 1.0e6, ALU.mult, ALU.add), t)
            t1 = dve(lambda e: e.tensor_tensor(SLS[:, 2 * b:2 * b + 2], RS[:, 12:14], RS[:, 10:12], ALU.add), t1)
            if "scat" not in streams:
                for i in range(2):
                    streams[f"scat{i}"] = streams.get(f"scat{i}") or Stream(sem(f"d_scat{i}"))
                streams["scat"] = streams["scat0"]
            for i in range(2):
                n = 2 * b + i
                st_ = streams[f"scat{i}"]
                st_.n += 16
                pool(lambda e, n=n, i=i, st_=st_: e.indirect_dma_start(
                    out=bufd, out_offset=bass.IndirectOffsetOnAxis(ap=SLS[:, n:n + 1], axis=0),
                    in_=XM[:, i, :], in_offset=None, bounds_check=EC - 1, oob_is_err=False).then_inc(st_.sem, 16),
                    t1, t_xm, t_zd, sig=False)
            sc_t[b] = [streams["scat0"].token(), streams["scat1"].token()]
            yield

        done2 = attention(1, m, x2d, lambda b: x2_t[b], epi1, done1)
        m.free()

        m = Mem()
        WG = [m(f"WG{i}", [128, 3, 2, 256], F32) for i in range(4)]
        XE = [m(f"XE{i}", [80, 2, D], F32) for i in range(2)]
        XET = [m(f"XET{i}", [128, 2, C], F32) for i in range(2)]
        SI = [m(f"SI{i}", [128, 2, C], F32) for i in range(2)]
        HE = [m(f"HE{i}", [128, 2, C], F32) for i in range(2)]
        YE = [m(f"YE{i}", [80, 2, D], F32) for i in range(2)]
        t_gg = dve(lambda e: e.tensor_scalar(GG[:, :], GG[:, :], tg[:, 3:4], None, ALU.mult), done2)
        tk = {}

        def load_w(e_):
            for i, n in enumerate(("weg", "weu", "wed")):
                tk["w", e_] = dma(sp, f"we{e_ % 4}", WG[e_ % 4][:, i, :, :],
                                  a[n][e_].rearrange("(k p) n -> p k n", p=128), done2, tk.get(("y", e_ - 4)))

        def load_x(e_):
            tk["x", e_] = dma(sp, f"xe{e_ % 2}", XE[e_ % 2][:, :, :],
                              bufd[e_ * C:(e_ + 1) * C, :].rearrange("(t p) d -> p t d", p=80),
                              done2, tk.get(("xt", e_ - 2)))

        def turn(e_):
            bk = e_ % 2
            for kt in range(2):
                for st in range(2):
                    p = pe(lambda e, kt=kt, st=st: e.transpose(
                        PS[:, bk, 160 * kt + 80 * st:160 * kt + 80 * st + 80],
                        XE[e_ % 2][:, st, 128 * kt:128 * kt + 128], ident[0:80, 0:80]),
                        tk["x", e_], bank_free[bk], sig=(kt + st == 2))
            tk["xt", e_] = p
            bank_free[bk] = tk["xet", e_] = act(lambda e: e.activation(
                XET[e_ % 2][:, :, :], PS[:, bk, 0:320].rearrange("p (k n) -> p k n", k=2), ACT.Copy),
                p, tk.get(("gu", e_ - 2)))

        def gate_up(e_):
            for i in range(2):
                bk = 2 + 2 * (e_ % 2) + i
                for mt in range(2):
                    for k in range(2):
                        p = pe(lambda e, i=i, mt=mt, k=k, bk=bk: e.matmul(
                            PS[:, bk, 160 * mt:160 * mt + 160], WG[e_ % 4][:, i, k, 128 * mt:128 * mt + 128],
                            XET[e_ % 2][:, k, :], start=(k == 0), stop=(k == 1)),
                            tk["xet", e_], tk["w", e_], bank_free[bk], sig=(mt + k == 2))
                if i == 0:
                    ts = act(lambda e, bk=bk: e.activation(
                        SI[e_ % 2][:, :, :], PS[:, bk, 0:320].rearrange("p (k n) -> p k n", k=2), ACT.Silu),
                        p, tk.get(("h", e_ - 2)))
                    bank_free[bk] = ts
                else:
                    tk["gu", e_] = p
                    bank_free[bk] = tk["h", e_] = dve(lambda e, bk=bk: e.tensor_tensor(
                        HE[e_ % 2][:, :, :], PS[:, bk, 0:320].rearrange("p (k n) -> p k n", k=2),
                        SI[e_ % 2][:, :, :], ALU.mult), p, ts, tk.get(("y", e_ - 2)))

        def down(e_):
            bk = 6 + e_ % 2
            for st in range(2):
                for k in range(2):
                    p = pe(lambda e, st=st, k=k: e.matmul(
                        PS[0:80, bk, 256 * st:256 * st + 256], HE[e_ % 2][:, k, 80 * st:80 * st + 80],
                        WG[e_ % 4][:, 2, k, :], start=(k == 0), stop=(k == 1)),
                        tk["h", e_], bank_free[bk], sig=(st + k == 2))
            tk["y", e_] = p
            bank_free[bk] = t = dve(lambda e: e.tensor_copy(
                YE[e_ % 2][:, :, :], PS[0:80, bk, :].rearrange("p (t n) -> p t n", t=2)), p, tk.get(("yd", e_ - 2)))
            tk["yd", e_] = dma(sp, f"y{e_ % 2}", yd[e_ * C:(e_ + 1) * C, :].rearrange("(t p) d -> p t d", p=80),
                               YE[e_ % 2][:, :, :], t)

        for e_ in range(3):
            load_w(e_)
        load_x(0)
        load_x(1)
        turn(0)
        for e_ in range(E):
            if e_ + 2 < E:
                pass
            gate_up(e_)
            if e_ + 1 < E:
                turn(e_ + 1)
            if e_ + 2 < E:
                load_x(e_ + 2)
            if e_ + 3 < E:
                load_w(e_ + 3)
            down(e_)
        yt = [tk["yd", E - 1], tk["yd", E - 2]]
        NG = 8
        GT = [m(f"GT{i}", [128, D], F32) for i in range(NG)]
        fin = {}
        for n in range(32):
            name = f"gat{n % NG}"
            if name not in streams:
                streams[name] = Stream(sem("d_" + name))
            st_ = streams[name]
            st_.n += 16
            pool(lambda e, n=n, st_=st_: e.indirect_dma_start(
                out=GT[n % NG][:, :], out_offset=None, in_=yd,
                in_offset=bass.IndirectOffsetOnAxis(ap=SLG[:, n:n + 1], axis=0),
                bounds_check=EC - 1, oob_is_err=False).then_inc(st_.sem, 16), yt, done2, fin.get(n - NG), sig=False)
            t = dve(lambda e, n=n: e.scalar_tensor_tensor(
                BASE[:, n, :], GT[n % NG][:, :], GG[:, n:n + 1], BASE[:, n, :], ALU.mult, ALU.add),
                (st_.sem, st_.n), t_gg)
            fin[n] = t
            if n % 4 == 3:
                dma(sp, "out", a["out"][128 * (n - 3):128 * (n + 1), :].rearrange("(t p) d -> p t d", p=128),
                    BASE[:, n - 3:n + 1, :], t)
        m.free()
        top.free()
        fix.free()
        ends = [s.token() for s in streams.values()]

        for s, v in ends:
            nc.sync.wait_ge(s, v)


def _inputs(i):
    f = np.ascontiguousarray
    order = np.arange(256).reshape(16, 16).T.reshape(-1)
    out = {
        "x": f(i["x"].reshape(T, D)),
        "ctxT": f(i["ctx_1024"].reshape(T, D).T),
        "g_xattn": f(i["g_xattn"]), "g_ffn": f(i["g_ffn"]),
        "b0": f(i["L0_xattn_b_proj"]), "b1": f(i["L1_xattn_bo"]),
        "wup": f(i["L0_ffn_w_up"]), "wgate": f(i["L0_ffn_w_gate"]), "wdown": f(i["L0_ffn_w_down"]),
        "wr": f(i["L1_ffn_w_router"]), "weg": f(i["L1_ffn_w_gate"]), "weu": f(i["L1_ffn_w_up"]),
        "wed": f(i["L1_ffn_w_down"]),
    }
    mask = i["mask_Bx1xSxS2_bk0"].reshape(NB, S, S)
    out["mq"] = f(mask)
    out["mt"] = f(mask.transpose(0, 2, 1))
    for layer, names in enumerate((("L0_xattn_W_q", "L0_xattn_W_k", "L0_xattn_W_v", "L0_xattn_W_proj"),
                                   ("L1_xattn_Wq", "L1_xattn_Wk", "L1_xattn_Wv", "L1_xattn_Wo"))):
        for n, name in zip("qkvo", names):
            w = i[name]
            out[f"w{n}{layer}"] = f((w[order] if n in "qk" else w).T)
    return out


def kernel(**inputs):
    import concourse.bacc as bacc
    from concourse.bass_utils import run_bass_kernel_spmd

    nc = bacc.Bacc("TRN2", target_bir_lowering=False, num_devices=1)
    arrays, aps = {}, {}
    for name, arr in _inputs({k: np.asarray(v) for k, v in inputs.items()}).items():
        arrays["in_" + name] = arr
        aps[name] = nc.dram_tensor("in_" + name, arr.shape, mybir.dt.from_np(arr.dtype), kind="ExternalInput").ap()
    aps["out"] = nc.dram_tensor("out_0", (T, D), F32, kind="ExternalOutput").ap()
    build(nc, aps)
    r = run_bass_kernel_spmd(nc, [arrays], core_ids=[0])
    return r.results[0]["out_0"].reshape(NB, S, D)
```

```python
from contextlib import ExitStack

import numpy as np
import concourse.bass as bass
from concourse import mybir

F32 = mybir.dt.float32
BF16 = mybir.dt.bfloat16
F16 = mybir.dt.float16
I16 = mybir.dt.int16
U16 = mybir.dt.uint16
I32 = mybir.dt.int32
U8 = mybir.dt.uint8
ALU = mybir.AluOpType
ACT = mybir.ActivationFunctionType
X = mybir.AxisListType.X

NB, S, D, H, HD = 16, 256, 256, 16, 16
T = NB * S
FF = 768
E, C = 32, 160
EC = E * C
NEG = -1.0e10
EPS = 1e-5
QMAX = 32767.0


class Queue:

    def __init__(self, eng, sem):
        self.eng, self.sem, self.n, self.seen = eng, sem, 0, {}

    def __call__(self, fn, *waits, sig=True):
        need = {}
        for w in flat(waits):
            if self.seen.get(id(w[0]), 0) < w[1]:
                self.seen[id(w[0])] = w[1]
                need[id(w[0])] = w
        for s, v in need.values():
            self.eng.wait_ge(s, v)
        ins = fn(self.eng)
        if not sig:
            return None
        self.n += 1
        ins.then_inc(self.sem, 1)
        return (self.sem, self.n)

    def wait(self, *waits):
        for s, v in flat(waits):
            if self.seen.get(id(s), 0) < v:
                self.seen[id(s)] = v
                self.eng.wait_ge(s, v)

    def last(self):
        return (self.sem, self.n)


def flat(ws):
    for w in ws:
        if w is None:
            continue
        if isinstance(w, list):
            yield from flat(w)
        else:
            yield w


def bc(ap, axis, n):
    shape = list(ap.shape)
    return ap.unsqueeze(axis).broadcast_to(shape[:axis] + [n] + shape[axis:])


class Stream:

    def __init__(self, sem):
        self.sem, self.n = sem, 0

    def token(self):
        return (self.sem, self.n) if self.n else None


def build(nc, a):
    ctx = ExitStack()
    with ctx:
        def sem(name):
            return ctx.enter_context(nc.semaphore(name))

        def dram(name, shape, dt):
            return nc.dram_tensor(name, shape, dt).ap()

        pe, act, dve, pool, sp = (Queue(g, sem(n)) for g, n in (
            (nc.tensor, "s_pe"), (nc.scalar, "s_act"), (nc.vector, "s_dve"), (nc.gpsimd, "s_pool"), (nc.sync, "s_sp")))
        streams = {}

        def dma(q, name, out, in_, *waits, **kw):
            if name not in streams:
                streams[name] = Stream(sem("d_" + name))
            st = streams[name]
            st.n += 16
            q(lambda e, st=st: e.dma_start(out, in_, **kw).then_inc(st.sem, 16), *waits, sig=False)
            return (st.sem, st.n)

        x1d = dram("x1d", (T, D), F32)
        x2d = dram("x2d", (T, D), F32)
        qd = dram("qd", (3, 3, 256, 256), BF16)
        kd = dram("kd", (3, 3, 256, 256), BF16)
        bufd = dram("bufd", (EC, D), F32)
        yd = dram("yd", (EC, D), F32)

        PS = ctx.enter_context(nc.psum_tensor("PS", [128, 8, 512], F32))
        bank_free = [None] * 8

        class Mem:

            count = 0

            def __init__(self):
                self.c = ExitStack()
                self.n = 0

            def __call__(self, name, shape, dt):
                Mem.count += 1
                return self.c.enter_context(nc.sbuf_tensor(f"{name}_{Mem.count}", shape, dt))

            def free(self):
                self.c.close()

        fix = Mem()
        ident = fix("ident", [128, 128], F32)
        identb = fix("identb", [128, 128], BF16)
        ones = fix("ones", [128, 128], F32)
        onesb = fix("onesb", [128, 128], BF16)
        triu = fix("triu", [128, 128], BF16)
        rev = fix("rev", [128, 8, 32], F32)
        gates = fix("gates", [128, 4], F32)
        tg = fix("tg", [128, 4], F32)
        bias_row = fix("bias_row", [128, 2, D], F32)
        tgb = fix("tgb", [128, 2, D], F32)
        mhalf = fix("mhalf", [128, 2], F32)
        sc = fix("sc", [128, 64], F32)
        wup = fix("wup", [128, 2, 2, FF], F16)
        wgt = fix("wgt", [128, 2, 2, FF], F16)
        wdn = fix("wdn", [128, 2, 6, D], F16)
        wsc = fix("wsc", [128, 3, 4], F32)
        t_wsc = {}

        t = [pool(lambda e, m=m, v=v: e.memset(m, v)) for m, v in (
            (ident[:, :], 0.0), (identb[:, :], 0.0), (ones[:, :], 1.0), (onesb[:, :], 1.0),
            (triu[:, :], 1.0), (mhalf[:, :], -0.5))]
        for m in (ident, identb):
            pool(lambda e, m=m: e.affine_select(out=m[:, :], in_=m[:, :], compare_op=ALU.not_equal, fill=1.0,
                                                base=0, pattern=[[-1, 128]], channel_multiplier=1), t)
        pool(lambda e: e.affine_select(out=triu[:, :], in_=triu[:, :], compare_op=ALU.is_ge, fill=0.0,
                                       base=0, pattern=[[1, 128]], channel_multiplier=-1), t)
        consts = pool(lambda e: e.iota(rev[:, :, :], pattern=[[0, 8], [-1, 32]], base=32, channel_multiplier=0,
                                       allow_small_or_imprecise_dtypes=True))
        g0 = dma(sp, "g", gates[:, 0:2], a["g_xattn"].rearrange("(o n) -> o n", o=1).broadcast_to([128, 2]))
        g0 = dma(sp, "g", gates[:, 2:4], a["g_ffn"].rearrange("(o n) -> o n", o=1).broadcast_to([128, 2]))
        g0 = dma(sp, "g", bias_row[:, 0, :], a["b0"].rearrange("(o n) -> o n", o=1).broadcast_to([128, D]))
        g0 = dma(sp, "g", bias_row[:, 1, :], a["b1"].rearrange("(o n) -> o n", o=1).broadcast_to([128, D]))
        t_tg = act(lambda e: e.activation(tg[:, :], gates[:, :], ACT.Tanh), g0)
        for i in range(2):
            t_tgb = pool(lambda e, i=i: e.tensor_scalar(tgb[:, i, :], bias_row[:, i, :], tg[:, i:i + 1], 0.0,
                                                        ALU.mult, ALU.add), t_tg, g0)

        def quantized_weights(m, bank):
            w = m("w_nat", [128, 1536], F32)
            q = m("w_q", [128, 512], I16)
            s = m("w_s", [128, 48], F32)
            r = m("w_r", [128, 48], F32)
            p = None
            for i, (n, dst, kt) in enumerate((("wup", wup, 2), ("wgate", wgt, 2), ("wdown", wdn, 6))):
                cols = 1536 // (kt * 128)
                ld = dma(sp, "wq", w[:, :].rearrange("p (m n) -> p m n", m=cols),
                         a[n].rearrange("(m p) n -> p m n", p=128), p, t_cr)
                yield from (None for _ in range(6))
                done = []
                for c in range(3):
                    f, g = slice(512 * c, 512 * c + 512), slice(16 * c, 16 * c + 16)
                    v = w[:, f].rearrange("p (b j) -> p b j", j=32)
                    t = dve(lambda e: e.tensor_reduce(s[:, g], v, X, ALU.max, apply_absolute_value=True), ld)
                    yield
                    t = dve(lambda e: e.tensor_scalar(s[:, g], s[:, g], 1.0 / 7.0, 1e-12, ALU.mult, ALU.max), t)
                    t = dve(lambda e: e.reciprocal(r[:, g], s[:, g]), t)
                    t = pool(lambda e: e.tensor_tensor(v, v, bc(r[:, g], 2, 32), ALU.mult), t)
                    yield from (None for _ in range(3))
                    t = dve(lambda e: e.tensor_scalar(q[:, :], w[:, f], 7.0, -8.0, ALU.min, ALU.max), t)
                    t = dve(lambda e: e.tensor_tensor(v, q[:, :].rearrange("p (b j) -> p b j", j=32),
                                                      bc(s[:, g], 2, 32), ALU.mult), t)
                    done.append(t)
                    yield
                t = dve(lambda e: e.tensor_reduce(wsc[:, i, 0:1], s[:, :], X, ALU.max), t)
                yield
                yield
                bk = bank()
                p = pe(lambda e: e.transpose(PS[0:1, bk, 0:128], wsc[:, i, 0:1], ident[:, :]), t, consts, bank_free[bk])
                bank_free[bk] = t = dve(lambda e: e.tensor_reduce(wsc[0:1, i, 1:2], PS[0:1, bk, 0:128], X, ALU.max), p)
                yield
                yield
                bk = bank()
                p = pe(lambda e: e.matmul(PS[:, bk, 0:1], ones[0:1, :], wsc[0:1, i, 1:2], start=True, stop=True),
                       t, bank_free[bk])
                bank_free[bk] = t = dve(lambda e: e.tensor_scalar(wsc[:, i, 2:3], PS[:, bk, 0:1], 7.0 / 16384.0, None,
                                                                  ALU.mult), p)
                t_wsc[i] = dve(lambda e: e.reciprocal(wsc[:, i, 3:4], wsc[:, i, 2:3]), t)
                for k in range(kt):
                    for mt in range(0, cols, 2):
                        yield
                        bk = bank()
                        for j in range(2):
                            src = w[:, (mt + j) * kt * 128 + k * 128:(mt + j) * kt * 128 + (k + 1) * 128]
                            p = pe(lambda e: e.transpose(PS[:, bk, 128 * j:128 * j + 128], src, ident[:, :]),
                                   done, consts, bank_free[bk])
                        hi, lo = (dst[:, j, k, mt * 128:(mt + 2) * 128] for j in range(2))
                        t = act(lambda e: e.activation(hi, PS[:, bk, 0:256], ACT.Copy, scale=wsc[:, i, 3:4]), p, t_wsc[i])
                        bank_free[bk] = dve(lambda e: e.scalar_tensor_tensor(
                            lo, PS[:, bk, 0:256], wsc[:, i, 3:4], hi, ALU.mult, ALU.subtract), t)

        def all_done():
            t = [q.last() for q in (pe, act, dve, pool) if q.n] + [s.token() for s in streams.values()]
            for q in (pe, act, dve, pool, sp):
                q.wait(t)
            return t

        scn = [0]

        def scalar_col(n=1):
            c = scn[0]
            scn[0] += n
            return c

        def global_scale(col, ncols, src, *waits):
            c = scalar_col(3)
            t = dve(lambda e: e.tensor_reduce(sc[:, c:c + 1], src, X, ALU.max, apply_absolute_value=True), *waits)
            p = pe(lambda e: e.transpose(PS[0:1, 7, 0:128], sc[:, c:c + 1], ident[:, :]), t, consts, bank_free[7])
            t = dve(lambda e: e.tensor_reduce(sc[0:1, c + 1:c + 2], PS[0:1, 7, 0:128], X, ALU.max), p)
            p = pe(lambda e: e.matmul(PS[:, 7, 128:129], ones[0:1, :], sc[0:1, c + 1:c + 2], start=True, stop=True), t)
            t = dve(lambda e: e.tensor_scalar(sc[:, c:c + 1], PS[:, 7, 128:129], 1.0 / QMAX, 1e-12,
                                              ALU.mult, ALU.max), p)
            bank_free[7] = t
            t = dve(lambda e: e.reciprocal(sc[:, c + 2:c + 3], sc[:, c:c + 1]), t)
            return sc[:, c:c + 1], sc[:, c + 2:c + 3], t

        crd = dram("crd", (8, 2048), F32)
        cm = Mem()
        cr = cm("cr", [64, 2048], F32)
        pair = float(np.array([0x3F803F80], np.uint32).view(np.float32)[0])
        t = [dve(lambda e: e.memset(cr[0:32, :], pair)), dve(lambda e: e.memset(cr[32:33, :], 0.0))]
        dma(sp, "cr", crd[0:4, :], cr[0:4, :], t)
        dma(sp, "cr", crd[5:8, :], cr[5:8, :])
        t_cr = dma(sp, "cr", crd[4:5, :], cr[32:33, :])
        cm.free()

        def layer_norm(tag, x, out, st, t_x, nb, extra=None, free=None):
            for i in range(2):
                t = dve(lambda e, i=i: e.bn_stats(st[:, 16 + 6 * i:22 + 6 * i], x[:, i, :]), t_x, free)
            for i in range(2):
                t = dve(lambda e, i=i: e.bn_aggr(st[:, 2 * i:2 * i + 2], st[:, 16 + 6 * i:22 + 6 * i]), t)
            mv = st[:, 0:4].rearrange("p (t k) -> p t k", k=2)
            t1 = dve(lambda e: e.tensor_scalar(st[:, 4:6], mv[:, :, 0], -1.0, None, ALU.mult), t)
            t2 = dve(lambda e: e.tensor_scalar(st[:, 6:8], mv[:, :, 1], EPS, None, ALU.add), t)
            t = pool(lambda e: e.tensor_tensor(st[:, 8:10], st[:, 6:8], mhalf[:, :], ALU.pow), t2, consts)
            if extra is not None:
                t = pool(lambda e: e.tensor_tensor(st[:, 8:10], st[:, 8:10], extra[0], ALU.mult), t, extra[1])
            yield
            yield
            for i in range(2):
                t = dve(lambda e, i=i: e.tensor_scalar(out[:, i, :], x[:, i, :], st[:, 4 + i:5 + i],
                                                       st[:, 8 + i:9 + i], ALU.add, ALU.mult), t, t1, free)
            return t

        def attention(L, m, xin, t_xin, epilogue, keep):
            XB = [m(f"XB{i}", [128, 2, D], F32) for i in range(5)]
            XN = m("XN", [128, 2, D], F32)
            ST = [m(f"ST{i}", [128, 32], F32) for i in range(2)]
            XT = m("XT", [128, 2, 256], F32)
            CT = [m(f"CT{i}", [128, 2, 256], F32) for i in range(2)]
            W = {n: m("W" + n, [128, 2, D], F32) for n in "qkvo"}
            QF = m("QF", [128, 512], F32)
            R1 = m("R1", [128, 512], F32)
            PP = [m(f"PP{i}", [128, 2, 3, 256], BF16) for i in range(2)]
            QS = [m(f"QS{i}", [100, H, 256], BF16) for i in range(3)]
            KS = [m(f"KS{i}", [100, H, 256], BF16) for i in range(3)]
            V = [m(f"V{i}", [128, 2, H, 32], F32) for i in range(3)]
            P = [m(f"P{i}", [128, 2, 256], F32) for i in range(4)]
            OT = [m(f"OT{i}", [128, 4, 256], F32) for i in range(2)]
            ON = m("ON", [128, 2, 256], F32)
            ONT = m("ONT", [128, 2, 256], F32)
            RD = m("RD", [128, 2, H], F32)
            NM = [m(f"NM{i}", [128, 2, H], F32) for i in range(2)]
            NH = m("NH", [128, 2, 2, 8], BF16)
            NR = m("NR", [128, 2, 8], F32)
            NP = m("NP", [128, 2, 3, 8], F32)
            NT = [m(f"NT{i}", [24, 256], BF16) for i in range(2)]
            if L == 0:
                MQ = [m(f"MQ{i}", [128, 2, 256], U8) for i in range(2)]
                MT = [m(f"MT{i}", [128, 2, 256], U8) for i in range(2)]
                AV = [m(f"AV{i}", [128, 2], F32) for i in range(2)]
                NQ = [m(f"NQ{i}", [128, 2, 256], BF16) for i in range(4)]
                MX = m("MX", [128, 4, 256], BF16)
                NK = [m(f"NK{i}", [128, 2, 256], BF16) for i in range(4)]
            for n in "qkvo":
                t_w = dma(sp, f"w{L}", W[n][:, :, :], a[f"w{n}{L}"].rearrange("(k p) n -> p k n", p=128), keep)
            for i in range(3):
                dma(sp, f"init{L}", QS[i][96:100, :, :].rearrange("p h n -> p (h n)").bitcast(F32), crd[0:4, :], keep, t_cr)
                t_ir = dma(sp, f"init{L}", KS[i][96:100, :, :].rearrange("p h n -> p (h n)").bitcast(F32), crd[4:8, :])
                t = pool(lambda e: e.memset(V[i][:, :, :, 16:32], 0.0), keep, t_cr)
                t_iv = pool(lambda e: e.memset(V[i][:, :, :, 16:17], 1.0), t)
            init = [t_ir, t_iv]
            misc = [0]
            tok = {}
            live = []
            spawn = live.append

            def bank():
                misc[0] ^= 1
                return 6 + misc[0]

            def g(k, b):
                return tok.get((k, b))

            def put(k, b, v):
                tok[(k, b)] = v

            def load(b):
                i = b % 5
                put("x", b, dma(sp, f"x{L}{i}", XB[i][:, :, :], xin[b * S:(b + 1) * S, :].rearrange(
                    "(t p) d -> p t d", p=128), keep, t_xin(b), g("xfree", b - 5)))
                j = b % 2
                put("ct", b, dma(sp, f"c{L}{j}", CT[j][:, :, :], a["ctxT"][:, b * S:(b + 1) * S].rearrange(
                    "(k p) n -> p k n", p=128), keep, g("ctfree", b - 2)))
                if L == 0:
                    put("m", b, [dma(sp, f"m{j}", MQ[j][:, :, :], a["mq"][b].rearrange("(t p) n -> p t n", p=128),
                                     keep, g("mfree", b - 2)),
                                 dma(sp, f"m{j}", MT[j][:, :, :], a["mt"][b].rearrange("(t p) n -> p t n", p=128),
                                     keep, g("mfree", b - 2))])

            def gap(n):
                for _ in range(n):
                    yield

            def split(which, b, bk, p, scale):
                n = 0 if which == "q" else 1
                pp, qf_, r1_ = PP[n], QF, R1
                st = (QS if which == "q" else KS)[b % 3]
                dd = (qd if which == "q" else kd)[b % 3]
                bankv = PS[:, bk, :]
                qf = qf_[:, :].rearrange("p (m n) -> p m n", m=2)
                r1 = r1_[:, :].rearrange("p (m n) -> p m n", m=2)
                t1 = act(lambda e: e.activation(qf_[:, :], bankv, ACT.Copy, scale=scale), p, g("r1", 0))
                th = act(lambda e: e.activation(pp[:, :, 0, :], bankv.rearrange("p (m n) -> p m n", m=2), ACT.Copy,
                                                scale=scale), g(which + "sent", b - 1))
                bank_free[bk] = th
                t = pool(lambda e: e.tensor_tensor(r1, qf, pp[:, :, 0, :], ALU.subtract), t1, th, g("lo", 0))
                put("r1", 0, t)
                yield from gap(2)
                t = dve(lambda e: e.tensor_copy(pp[:, :, 1, :], r1), t)
                t = pool(lambda e: e.tensor_tensor(pp[:, :, 2, :], r1, pp[:, :, 1, :], ALU.subtract), t)
                put("lo", 0, t)
                yield from gap(2)
                for part in range(3):
                    sent = dma(sp, f"{which}w", dd[part].rearrange("(m p) n -> p m n", p=128), pp[:, :, part, :],
                               t, g(which + "st", b - 3))
                put(which + "sent", b, sent)
                yield from gap(2)
                free = [g("c", b - 3), g("bdone", b - 3), init]
                flatd = dd.rearrange("s (r h) n -> s r (h n)", h=H)

                def stack(row, part, k=1):
                    dst = st[row:row + 16 * k, :, :].rearrange("p h n -> p (h n)")
                    src = flatd[part] if k == 1 else flatd[part:part + k].rearrange("s r n -> (s r) n")
                    return dma(sp, f"{which}s{b % 3}", dst, src, sent, free)

                if which == "q":
                    stack(0, 0, 3)
                    stack(48, 0, 2)
                    tt = stack(80, 0)
                else:
                    for s_, part in enumerate((0, 0, 0, 1, 1, 2)):
                        tt = stack(16 * s_, part)
                put(which + "st", b, tt)

            def project(w, src, bk, t):
                for mt in range(2):
                    for k in range(2):
                        p = pe(lambda e, mt=mt, k=k: e.matmul(
                            PS[:, bk, 256 * mt:256 * mt + 256], W[w][:, k, 128 * mt:128 * mt + 128], src[:, k, :],
                            start=(k == 0), stop=(k == 1)), t, t_w, bank_free[bk], sig=(mt + k == 2))
                return p

            def stN(b):
                j = b % 2
                ex = None
                if L == 0:
                    t = dve(lambda e: e.tensor_reduce(AV[j][:, :], MQ[j][:, :, :], X, ALU.max), g("m", b), g("xn", b - 2))
                    ex = (AV[j][:, :], t)
                    pool(lambda e: e.tensor_scalar(NQ[b % 4][:, :, :], MQ[j][:, :, :], -1.0, -NEG, ALU.add, ALU.mult),
                         g("m", b), g("bmax", b - 4))
                    tn = pool(lambda e: e.tensor_scalar(NK[b % 4][:, :, :], MT[j][:, :, :], -1.0, -NEG, ALU.add,
                                                        ALU.mult), g("c", b - 4))
                    put("mfree", b, [tn, t])
                    put("pen", b, tn)
                yield
                t = yield from layer_norm("a", XB[b % 5], XN, ST[j], g("x", b), b, ex, [g("xtr", b - 1), g("xn", b - 2)])
                put("xn", b, t)
                put("xb", b, pool(lambda e: e.tensor_tensor(
                    XB[b % 5][:, :, :], XB[b % 5][:, :, :], bc(tgb[:, L, :], 1, 2), ALU.add),
                    t, t_tgb))

            def stA(b):
                j = b % 2
                ct = CT[j]
                bk = bank()
                p = project("k", ct, bk, g("ct", b))
                spawn(split("k", b, bk, p, 1.0))
                t = g("xn", b)
                yield
                yield from gap(2)
                bk = bank()
                for kt in range(2):
                    for tt in range(2):
                        p = pe(lambda e, kt=kt, tt=tt: e.transpose(
                            PS[:, bk, 256 * kt + 128 * tt:256 * kt + 128 * tt + 128],
                            XN[:, tt, 128 * kt:128 * kt + 128], ident[:, :]), t, consts, bank_free[bk], sig=(kt + tt == 2))
                put("xtr", b, p)
                bank_free[bk] = t = act(lambda e: e.activation(
                    XT[:, :, :], PS[:, bk, :].rearrange("p (k n) -> p k n", k=2), ACT.Copy), p, g("qp", b - 1))
                yield from gap(2)
                bk = bank()
                p = project("q", XT, bk, t)
                put("qp", b, p)
                spawn(split("q", b, bk, p, 0.25))
                yield from gap(4)
                bk = bank()
                for tt in range(2):
                    for k in range(2):
                        p = pe(lambda e, tt=tt, k=k: e.matmul(
                            PS[:, bk, 256 * tt:256 * tt + 256], ct[:, k, 128 * tt:128 * tt + 128], W["v"][:, k, :],
                            start=(k == 0), stop=(k == 1)), g("ct", b), bank_free[bk], sig=(tt + k == 2))
                put("ctfree", b, p)
                bank_free[bk] = act(lambda e: e.activation(
                    V[b % 3][:, :, :, 0:16], PS[:, bk, :].rearrange("p (t h r) -> p t h r", t=2, h=H), ACT.Copy),
                    p, g("av", b - 3), init)
                put("v", b, bank_free[bk])

            def stB(b):
                Q, K = QS[b % 3], KS[b % 3]
                nm = NM[b % 2]
                for h in range(H):
                    bk = 2 + h % 2
                    for qt in range(2):
                        o = PS[:, bk, 256 * qt:256 * qt + 256]
                        p = pe(lambda e, o=o, h=h, qt=qt: e.matmul(
                            o, Q[0:96, h, 128 * qt:128 * qt + 128], K[0:96, h, :], start=True, stop=True),
                            g("qst", b), g("kst", b), bank_free[bk], sig=(qt == 1))
                    if L == 0:
                        for qt in range(2):
                            t = dve(lambda e: e.tensor_tensor_reduce(
                                MX[:, 2 * (h % 2) + qt, :], PS[:, bk, 256 * qt:256 * qt + 256], NQ[b % 4][:, qt, :], -1.0, 1.0e30,
                                ALU.add, ALU.min, nm[:, qt, h:h + 1]), p, g("pen", b), g("nm", b - 2), g("mx", 2 * (h % 2) + qt))
                            put("mx", 2 * (h % 2) + qt, t)
                        bank_free[bk] = t
                    else:
                        bank_free[bk] = dve(lambda e, h=h, bk=bk: e.tensor_reduce(
                            nm[:, :, h], PS[:, bk, :].rearrange("p (t n) -> p t n", t=2), X, ALU.max, negate=True),
                            p, g("nm", b - 2))
                    put("bmax", b, bank_free[bk])
                    if h == H - 1:
                        put("bdone", b, p)
                    if h % 8 == 7:
                        spawn(maxima(b, h // 8, bank_free[bk]))
                    yield

            def maxima(b, hh, t):
                Q, nm = QS[b % 3], NM[b % 2]
                v = nm[:, :, 8 * hh:8 * hh + 8]
                yield
                t = pool(lambda e: e.tensor_copy(NH[:, 0, :, :], v), t)
                pool(lambda e: e.tensor_copy(NP[:, :, 0, :], NH[:, 0, :, :]), t, g("ntr", 0))
                t = pool(lambda e: e.tensor_tensor(NR[:, :, :], v, NH[:, 0, :, :], ALU.subtract), t)
                t = pool(lambda e: e.tensor_copy(NH[:, 1, :, :], NR[:, :, :]), t)
                pool(lambda e: e.tensor_copy(NP[:, :, 1, :], NH[:, 1, :, :]), t)
                t = pool(lambda e: e.tensor_tensor(NP[:, :, 2, :], NR[:, :, :], NH[:, 1, :, :], ALU.subtract), t)
                if hh == 1:
                    put("nm", b, t)
                yield from gap(2)
                mb = bank()
                for qt in range(2):
                    p = pe(lambda e, qt=qt: e.transpose(
                        PS[0:24, mb, 128 * qt:128 * qt + 128],
                        NP[:, qt, :, :].rearrange("p a h -> p (a h)"), ident[:, :]),
                        t, consts, bank_free[mb], sig=(qt == 1))
                put("ntr", 0, p)
                nt = NT[hh]
                bank_free[mb] = t = act(lambda e: e.activation(nt[:, :], PS[0:24, mb, 0:256], ACT.Copy),
                                        p, g("nsent%d" % hh, 0))
                for part in range(3):
                    s = dma(sp, f"n{hh}{b % 3}", Q[97 + part:98 + part, 8 * hh:8 * hh + 8, :],
                            nt[8 * part:8 * part + 8, :], t, g("c", b - 3), init)
                put("nsent%d" % hh, 0, s)
                put("nst%d" % hh, b, s)

            def av(b, h):
                gi, i = h // 4, h % 4
                ob = 4 + h // 8
                for kt in range(2):
                    p = pe(lambda e, kt=kt: e.matmul(
                        PS[32 * i:32 * i + 32, ob, 256 * (gi % 2):256 * (gi % 2) + 256],
                        V[b % 3][:, kt, h, :], P[h % 4][:, kt, :], start=(kt == 0), stop=(kt == 1)),
                        g("p", (b, h)), g("v", b), bank_free[ob] if h % 8 == 0 else None, sig=(kt == 1))
                put("avp", h % 4, p)
                if h == H - 1:
                    put("av", b, p)
                if h % 8 == 7:
                    hh = h // 8
                    bank_free[ob] = act(lambda e: e.activation(
                        OT[b % 2][:, 2 * hh:2 * hh + 2, :], PS[:, ob, :].rearrange("p (g n) -> p g n", g=2), ACT.Copy),
                        p, g("otr", b - 2))
                    put("ot", b, bank_free[ob])

            def stC(b):
                Q, K = QS[b % 3], KS[b % 3]
                for h in range(H):
                    bk = h % 2
                    for kt in range(2):
                        o = PS[:, bk, 256 * kt:256 * kt + 256]
                        p = pe(lambda e, o=o, h=h, kt=kt: e.matmul(
                            o, K[0:100, h, 128 * kt:128 * kt + 128], Q[0:100, h, :], start=True, stop=(L == 1)),
                            g("nst%d" % (h // 8), b), bank_free[bk], sig=(L == 1 and kt == 1))
                        if L == 0:
                            p = pe(lambda e, o=o, kt=kt: e.matmul(o, identb[:, :], NK[b % 4][:, kt, :], start=False,
                                                                  stop=True), g("pen", b), sig=(kt == 1))
                    if h == H - 1:
                        put("c", b, p)
                    bank_free[bk] = act(lambda e, h=h, bk=bk: e.activation(
                        P[h % 4][:, :, :], PS[:, bk, :].rearrange("p (k n) -> p k n", k=2), ACT.Exp), p,
                        g("avp", h % 4))
                    put("p", (b, h), bank_free[bk])
                    if h >= 2:
                        av(b, h - 2)
                    yield

            def stD(b):
                av(b, H - 2)
                yield
                av(b, H - 1)
                yield from gap(2)
                for qt in range(2):
                    bk = bank()
                    for gi in range(4):
                        p = pe(lambda e, gi=gi, qt=qt, bk=bk: e.transpose(
                            PS[:, bk, 128 * gi:128 * gi + 128], OT[b % 2][:, gi, 128 * qt:128 * qt + 128],
                            ident[:, :]), g("ot", b), bank_free[bk], sig=(gi == 3))
                    pv = PS[:, bk, :].rearrange("p (h r) -> p h r", r=32)
                    t = dve(lambda e, qt=qt, pv=pv: e.reciprocal(RD[:, qt, :], pv[:, :, 16]), p)
                    bank_free[bk] = t = dve(lambda e, qt=qt, pv=pv: e.tensor_tensor(
                        ON[:, qt, :].rearrange("p (h r) -> p h r", r=16), pv[:, :, 0:16],
                        bc(RD[:, qt, :], 2, 16), ALU.mult), t, g("ontr", b - 1))
                    if qt == 1:
                        put("otr", b, p)
                    yield
                yield from gap(2)
                bk = bank()
                for kt in range(2):
                    for qt in range(2):
                        p = pe(lambda e, kt=kt, qt=qt: e.transpose(
                            PS[:, bk, 256 * kt + 128 * qt:256 * kt + 128 * qt + 128],
                            ON[:, qt, 128 * kt:128 * kt + 128], ident[:, :]), t, bank_free[bk], sig=(kt + qt == 2))
                put("ontr", b, p)
                bank_free[bk] = t = act(lambda e: e.activation(
                    ONT[:, :, :], PS[:, bk, :].rearrange("p (k n) -> p k n", k=2), ACT.Copy), p, g("op", b - 1))
                yield from gap(2)
                bk = bank()
                for qt in range(2):
                    for k in range(2):
                        p = pe(lambda e, qt=qt, k=k: e.matmul(
                            PS[:, bk, 256 * qt:256 * qt + 256], ONT[:, k, 128 * qt:128 * qt + 128],
                            W["o"][:, k, :], start=(k == 0), stop=(k == 1)), t, bank_free[bk], sig=(qt + k == 2))
                put("op", b, p)
                xb = XB[b % 5]
                bank_free[bk] = t = dve(lambda e: e.scalar_tensor_tensor(
                    xb[:, :, :], PS[:, bk, :].rearrange("p (t n) -> p t n", t=2), tg[:, L:L + 1], xb[:, :, :],
                    ALU.mult, ALU.add), p, g("xb", b), t_tg)
                yield
                yield from epilogue(b, xb, t, bank, ST[b % 2], g, put)

            for s in range(-3, NB + 3):
                if 0 <= s + 3 < NB:
                    load(s + 3)
                if 0 <= s < NB:
                    spawn(stC(s))
                if 0 <= s + 1 < NB:
                    spawn(stB(s + 1))
                if 0 <= s + 2 < NB:
                    spawn(stA(s + 2))
                if 0 <= s - 1 < NB:
                    spawn(stD(s - 1))
                for slot in range(16 if s > -3 else 8):
                    if slot == (8 if s > -3 else 0) and 0 <= s + 3 < NB:
                        spawn(stN(s + 3))
                    live[:] = [x for x in live if next(x, "end") != "end"]
                if L == 0 and s == 0:
                    spawn(quantized_weights(m, bank))
            assert not live
            return all_done()

        top = Mem()
        XNT = top("XNT", [128, 2, T], F32)
        AM = top("AM", [128, 96], F32)
        m = Mem()
        XM = m("XM", [128, 2, D], F32)
        ST0 = m("ST0", [128, 32], F32)

        def epi0(b, xb, t, bank, st, g, put):
            put("x1", b, dma(sp, f"x1{b % 4}", x1d[b * S:(b + 1) * S, :].rearrange("(t p) d -> p t d", p=128),
                             xb[:, :, :], t))
            t = yield from layer_norm("e", xb, XM, ST0, t, b, None, [g("xmtr", b - 1), g("xm", b - 1)])
            put("xm", b, t)
            put("xfree", b, [t, g("x1", b)])
            for _ in range(2):
                yield
            bk = bank()
            for kt in range(2):
                for tt in range(2):
                    p = pe(lambda e, kt=kt, tt=tt: e.transpose(
                        PS[:, bk, 256 * kt + 128 * tt:256 * kt + 128 * tt + 128],
                        XM[:, tt, 128 * kt:128 * kt + 128], ident[:, :]), t, bank_free[bk], sig=(kt + tt == 2))
            put("xmtr", b, p)
            dst = XNT[:, :, b * S:(b + 1) * S]
            bank_free[bk] = t = act(lambda e: e.activation(
                dst, PS[:, bk, :].rearrange("p (k n) -> p k n", k=2), ACT.Copy), p)
            yield
            yield
            t_am[0] = dve(lambda e: e.tensor_reduce(AM[:, b:b + 1], dst, mybir.AxisListType.XY, ALU.max,
                                                    apply_absolute_value=True), t)
            x1_t[b] = g("x1", b)
            yield

        t_am, x1_t = [None], {}
        done0 = attention(0, m, a["x"], lambda b: None, epi0, t_cr)
        m.free()

        m = Mem()
        G = m("G", [128, 6, T], F32)
        UQ = m("UQ", [128, 6, T], I16)
        Gf = G[:, :, :].rearrange("p m n -> p (m n)")
        UQf = UQ[:, :, :].rearrange("p m n -> p (m n)")
        s1, i1, t = global_scale(0, 16, AM[:, 0:16], t_am[0])
        PARTS = ((0, 0), (0, 1), (1, 0))
        XH = XNT[:, :, :].bitcast(F16)
        tq, tqi = {}, {}
        for n in range(9):
            if n < 8:
                tqi[n] = dve(lambda e: e.tensor_scalar(UQ[:, 0:2, 512 * n:512 * n + 512], XNT[:, :, 512 * n:512 * n + 512],
                                                       i1, QMAX, ALU.mult, ALU.min), t, done0)
            if n:
                hi, lo = (XH[:, :, 1024 * n - 1024 + 512 * j:1024 * n - 512 + 512 * j] for j in range(2))
                q = UQ[:, 0:2, 512 * n - 512:512 * n]
                th = act(lambda e: e.activation(hi, q, ACT.Copy), tqi[n - 1])
                tq[n - 1] = dve(lambda e: e.tensor_tensor(lo, q, hi, ALU.subtract), th)
        us = scalar_col(2)
        us, gs = sc[:, us:us + 1], sc[:, us + 1:us + 2]
        t_us = dve(lambda e: e.tensor_tensor(us, s1, wsc[:, 0, 2:3], ALU.mult), t)
        t_us = dve(lambda e: e.tensor_tensor(gs, s1, wsc[:, 1, 2:3], ALU.mult), t)

        def ff_in(w, scale, wait, col):
            out = None
            for n in range(8):
                for mt in range(6):
                    bk = (n * 6 + mt) % 7
                    for j, (wp, xp) in enumerate(PARTS * 2):
                        k = j // 3
                        p = pe(lambda e: e.matmul(
                            PS[:, bk, :], w[:, wp, k, 128 * mt:128 * mt + 128],
                            XH[:, k, 1024 * n + 512 * xp:1024 * n + 512 * xp + 512],
                            start=(j == 0), stop=(j == 5)), tq[n], bank_free[bk], sig=(j == 5))
                    dst = G[:, mt, 512 * n:512 * n + 512]
                    bank_free[bk] = t = act(lambda e: e.activation(dst, PS[:, bk, :], ACT.Copy, scale=scale), p,
                                            t_us, wait(mt, n))
                    c = n * 6 + mt
                    out = dve(lambda e, dst=dst, c=c: e.tensor_reduce(
                        AM[:, col + c:col + c + 1], dst, X, ALU.max, apply_absolute_value=True), t)
            return out

        t = ff_in(wup, us, lambda mt, n: None, 48 * 0)
        s2, i2, t = global_scale(0, 48, AM[:, 0:48], t)
        tu = {}
        for n in range(8):
            v, q = G[:, :, 512 * n:512 * n + 512], UQ[:, :, 512 * n:512 * n + 512]
            tu[n] = dve(lambda e, v=v, q=q: e.tensor_scalar(q, v, i2, QMAX, ALU.mult, ALU.min), t, tq[7])
        t = ff_in(wgt, gs, lambda mt, n: tu[n], 48)
        s3, i3, t = global_scale(0, 48, AM[:, 48:96], t)
        NCH = 24
        CW = 6 * T // NCH
        XNf = XNT[:, :, :].rearrange("p k n -> p (k n)")
        GQ = [XNf[:, 512 * i:512 * i + 512].bitcast(I16) for i in range(3)]
        SG = [XNf[:, 1536 + 1024 * i:2560 + 1024 * i] for i in range(3)]
        SQ = [XNf[:, 4608 + 512 * i:5120 + 512 * i].bitcast(U16) for i in range(3)]
        t0, tsg, tsq, tgs = t, {}, {}, {}
        for c in range(NCH + 3):
            if c < NCH:
                v = Gf[:, CW * c:CW * c + CW]
                t = act(lambda e: e.activation(GQ[c % 3], v, ACT.Copy, scale=i3), t0, pe.last(), tgs.get(c - 3))
                tsg[c] = act(lambda e: e.activation(SG[c % 3], GQ[c % 3], ACT.Sigmoid, scale=s3), t, tsq.get(c - 3))
            k = c - 1
            if 0 <= k < NCH:
                tsq[k] = pool(lambda e: e.tensor_scalar(SQ[k % 3], SG[k % 3], 65536.0, 0.0, ALU.mult, ALU.add),
                              tsg[k], tgs.get(k - 3))
            k = c - 2
            if 0 <= k < NCH:
                v = Gf[:, CW * k:CW * k + CW]
                tgs[k] = dve(lambda e: e.tensor_tensor_reduce(v, GQ[k % 3], SQ[k % 3], s3, -1.0e30, ALU.mult, ALU.max,
                                                              AM[:, k:k + 1]), tsq[k])
            k = c - 3
            if 0 <= k < NCH:
                v = Gf[:, CW * k:CW * k + CW]
                t = dve(lambda e: e.tensor_scalar(v, v, 1.0, None, ALU.mult, ALU.min, accum_out=AM[:, 24 + k:25 + k]),
                        tgs[k])
        s4, i4, t0 = global_scale(0, NCH, AM[:, 0:2 * NCH], t)
        tgq, tpr = {}, {}
        for c in range(NCH + 2):
            if c < NCH:
                v = Gf[:, CW * c:CW * c + CW]
                tgq[c] = act(lambda e: e.activation(GQ[c % 3], v, ACT.Copy, scale=i4), t0, tpr.get(c - 3))
            k = c - 1
            if 0 <= k < NCH:
                v, u = Gf[:, CW * k:CW * k + CW], UQf[:, CW * k:CW * k + CW]
                tpr[k] = dve(lambda e: e.tensor_tensor_reduce(v, GQ[k % 3], u, 1.0, -1.0e30, ALU.mult, ALU.max,
                                                              AM[:, 48 + k:49 + k]), tgq[k])
            k = c - 2
            if 0 <= k < NCH:
                v = Gf[:, CW * k:CW * k + CW]
                t = dve(lambda e: e.tensor_scalar(v, v, 1.0, None, ALU.mult, ALU.min, accum_out=AM[:, 72 + k:73 + k]),
                        tpr[k])
        s5, i5, t = global_scale(0, NCH, AM[:, 48:48 + 2 * NCH], t)
        c = scalar_col(2)
        fs = sc[:, c:c + 1]
        t5 = dve(lambda e: e.tensor_scalar(fs, s5, s4, s2, ALU.mult, ALU.mult), t)
        t5 = dve(lambda e: e.tensor_scalar(fs, fs, tg[:, 2:3], 1.0 / 65536.0, ALU.mult, ALU.mult), t5)
        t5 = dve(lambda e: e.tensor_tensor(fs, fs, wsc[:, 2, 2:3], ALU.mult), t5)
        XD = [XNf[:, 6144 + 512 * i:6656 + 512 * i].rearrange("p (t n) -> p t n", t=2) for i in range(4)]
        x2_t = {}
        stt, tin, ld = {}, {}, {}

        GH = G[:, :, :].bitcast(F16)
        t_q = {}

        def down_quant(b):
            t_q[b] = dve(lambda e: e.tensor_scalar(UQ[:, :, 256 * b:256 * b + 256], G[:, :, 256 * b:256 * b + 256],
                                                   i5, QMAX, ALU.mult, ALU.min), t)

        def down_in(b):
            q = UQ[:, :, 256 * b:256 * b + 256]
            hi, lo = (GH[:, :, 512 * b + 256 * j:512 * b + 256 * j + 256] for j in range(2))
            t1 = act(lambda e: e.activation(hi, q, ACT.Copy), t_q[b])
            if b + 1 < NB:
                down_quant(b + 1)
            tin[b] = dve(lambda e: e.tensor_tensor(lo, q, hi, ALU.subtract), t1)
            ld[b] = dma(sp, f"xd{b % 4}", XD[b % 4], x1d[b * S:(b + 1) * S, :].rearrange(
                "(t p) d -> p t d", p=128), x1_t[b], stt.get(b - 4), t)

        down_quant(0)
        down_in(0)
        down_in(1)
        for b in range(NB):
            if b + 2 < NB:
                down_in(b + 2)
            bk = b % 7
            for tt in range(2):
                for j, (wp, xp) in enumerate(((0, 0), (1, 0), (0, 1)) * 6):
                    k = j // 3
                    c = 512 * b + 256 * xp + 128 * tt
                    p = pe(lambda e: e.matmul(
                        PS[:, bk, 256 * tt:256 * tt + 256], GH[:, k, c:c + 128], wdn[:, wp, k, :],
                        start=(j == 0), stop=(j == 17)), tin[b], bank_free[bk], sig=(tt == 1 and j == 17))
            bank_free[bk] = t2 = dve(lambda e: e.scalar_tensor_tensor(
                XD[b % 4], PS[:, bk, :].rearrange("p (t n) -> p t n", t=2), fs, XD[b % 4],
                ALU.mult, ALU.add), p, ld[b], t5)
            stt[b] = x2_t[b] = dma(sp, f"x2{b % 4}", x2d[b * S:(b + 1) * S, :].rearrange("(t p) d -> p t d", p=128),
                                   XD[b % 4], t2)
        done1 = all_done()
        m.free()
        top.free()

        top = Mem()
        BASE = top("BASE", [128, 32, D], F32)
        GG = top("GG", [128, 32], F32)
        SLG = top("SLG", [128, 32], I32)
        SLS = top("SLS", [128, 32], I32)
        m = Mem()
        XMS = m("XM1", [128, 2, 8, D], F32)
        ST0 = m("ST1", [128, 32], F32)
        XMT = m("XMT", [128, 2, 256], F32)
        WR = m("WR", [128, 2, E], F32)
        LG = m("LG", [128, 2, 8, E], F32)
        EX = m("EX", [128, 8, E], F32)
        OHF = m("OHF", [128, 8, E], F32)
        OHB = m("OHB", [128, 8, E], BF16)
        CN = m("CN", [128, 2, E], BF16)
        CS = m("CS", [128, E], F32)
        RS = m("RS", [128, 8, 8], F32)
        ZB = m("ZB", [128, D], F32)
        t_z = dve(lambda e: e.memset(ZB[:, :], 0.0), done1)
        for i in range(EC // 128 // 8):
            t_zd = dma(sp, "zero", bufd[1024 * i:1024 * i + 1024, :].rearrange("(t p) d -> p t d", p=128),
                       bc(ZB[:, :], 1, 8), t_z)
        t_c = dve(lambda e: e.memset(CN[:, :, :], 0.0), done1)
        t_wr = dma(sp, "wr", WR[:, :, :], a["wr"].rearrange("(k p) n -> p k n", p=128), done1)
        cn_t = [t_c]
        sc_t = {}
        rt_t = {}
        for i in range(2):
            streams[f"scat{i}"] = Stream(sem(f"d_scat{i}"))
        groups = [(0, 4), (4, 4), (8, 4), (12, 2), (14, 2)]
        group_of = {b: (n, b - b0, nb) for n, (b0, nb) in enumerate(groups) for b in range(b0, b0 + nb)}

        def epi1(b, xb, t, bank, st, g, put):
            n, at, nb = group_of[b]
            XM = XMS[:, n % 2, 2 * at:2 * at + 2, :]
            t = yield from layer_norm("e", xb, XM, ST0, t, b, None, [g("xm", b - 1), sc_t.get(n - 2)])
            put("xm", b, t)
            yield
            tb = dve(lambda e: e.scalar_tensor_tensor(BASE[:, 2 * b:2 * b + 2, :], XM, tg[:, 3:4],
                                                      xb[:, :, :], ALU.mult, ALU.add), t, done1)
            put("xfree", b, [t, tb])
            yield
            bk = bank()
            for kt in range(2):
                for tt in range(2):
                    p = pe(lambda e, kt=kt, tt=tt: e.transpose(
                        PS[:, bk, 256 * kt + 128 * tt:256 * kt + 128 * tt + 128],
                        XM[:, tt, 128 * kt:128 * kt + 128], ident[:, :]), t, bank_free[bk], sig=(kt + tt == 2))
            bank_free[bk] = t = act(lambda e: e.activation(
                XMT[:, :, :], PS[:, bk, :].rearrange("p (k n) -> p k n", k=2), ACT.Copy), p, g("rt", b - 1))
            yield
            yield
            bk = bank()
            for tt in range(2):
                for kt in range(2):
                    p = pe(lambda e, kt=kt, tt=tt: e.matmul(
                        PS[:, bk, 32 * tt:32 * tt + 32], XMT[:, kt, 128 * tt:128 * tt + 128], WR[:, kt, :],
                        start=(kt == 0), stop=(kt == 1)), t, t_wr, bank_free[bk], sig=(kt + tt == 2))
            put("rt", b, p)
            bank_free[bk] = act(lambda e: e.activation(
                LG[:, n % 2, 2 * at:2 * at + 2, :], PS[:, bk, 0:64].rearrange("p (t n) -> p t n", t=2), ACT.Copy),
                p, rt_t.get(n - 2))
            if at == nb - 1:
                t = bank_free[bk]
                yield
                yield from route(n, t, [g("xm", k) for k in range(b - at, b + 1)], bank)

        def route(n, t, t_xm, bank):
            b0, nb = groups[n]
            w = 2 * nb
            lg = LG[:, n % 2, 0:w, :]
            ex, ohf, ohb, rs = EX[:, 0:w, :], OHF[:, 0:w, :], OHB[:, 0:w, :], RS[:, :, 0:w]
            mx, sm, rv, ps, sl, ac = (rs[:, i, :] for i in range(6))
            t = dve(lambda e: e.tensor_reduce(mx, lg, X, ALU.max), t, rt_t.get(n - 1))
            t = dve(lambda e: e.tensor_tensor(ohf, lg, bc(mx, 2, E), ALU.subtract), t)
            te = act(lambda e: e.activation(ex, ohf, ACT.Exp), t)
            yield
            t = dve(lambda e: e.tensor_reduce(sm, ex, X, ALU.add), te)
            t_sm = dve(lambda e: e.reciprocal(sm, sm), t)
            t = dve(lambda e: e.scalar_tensor_tensor(ex, ohf, 0.0, rev[:, 0:w, :], ALU.is_equal, ALU.mult), t)
            t = dve(lambda e: e.tensor_reduce(rv, ex, X, ALU.max), t)
            t = dve(lambda e: e.tensor_tensor(ohb, rev[:, 0:w, :], bc(rv, 2, E), ALU.is_equal), t)
            tc = dve(lambda e: e.tensor_reduce(CS[:, :], ohb.rearrange("p t n -> p n t"), X, ALU.add), t)
            tc = dve(lambda e: e.tensor_tensor(CN[:, (n + 1) % 2, :], CN[:, n % 2, :], CS[:, :], ALU.add), tc, cn_t[0])
            cn_t0, cn_t[0] = cn_t[0], tc
            yield
            yield
            bk = bank()
            o = PS[:, bk, 0:32 * w].rearrange("p (t n) -> p t n", n=E)
            pe(lambda e: e.matmul(o, triu[:, :], ohb, start=True, stop=False), t, bank_free[bk], sig=False)
            for j in range(w - 1):
                pe(lambda e: e.matmul(o[:, j + 1:w, :], onesb[:, :], bc(ohb[:, j, :], 1, w - 1 - j),
                                      start=False, stop=False), sig=False)
            p = pe(lambda e: e.matmul(o, onesb[:, :], bc(CN[:, n % 2, :], 1, w), start=False, stop=True), cn_t0)
            bank_free[bk] = t = dve(lambda e: e.tensor_tensor(ohf, o, ohb, ALU.mult), p)
            t = dve(lambda e: e.tensor_reduce(ps, ohf, X, ALU.add), t)
            t = dve(lambda e: e.tensor_scalar(sl, rv, -float(C), float(C * E - 1), ALU.mult, ALU.add), t)
            ta = dve(lambda e: e.tensor_scalar(ac, ps, float(C), None, ALU.is_le), t)
            t = dve(lambda e: e.tensor_tensor(sl, sl, ps, ALU.add), t)
            t = dve(lambda e: e.tensor_tensor(sl, sl, ac, ALU.mult), t, ta)
            dve(lambda e: e.tensor_tensor(GG[:, 2 * b0:2 * b0 + w], ac, sm, ALU.mult), ta, t_sm)
            dve(lambda e: e.tensor_copy(SLG[:, 2 * b0:2 * b0 + w], sl), t)
            t1 = dve(lambda e: e.tensor_scalar(ac, ac, -1.0e6, 1.0e6, ALU.mult, ALU.add), t)
            t1 = dve(lambda e: e.tensor_tensor(SLS[:, 2 * b0:2 * b0 + w], sl, ac, ALU.add), t1)
            rt_t[n] = t1
            for i in range(w):
                st_ = streams[f"scat{n % 2}"]
                st_.n += 16
                pool(lambda e: e.indirect_dma_start(
                    out=bufd, out_offset=bass.IndirectOffsetOnAxis(ap=SLS[:, 2 * b0 + i:2 * b0 + i + 1], axis=0),
                    in_=XMS[:, n % 2, i, :], in_offset=None, bounds_check=EC - 1,
                    oob_is_err=False).then_inc(st_.sem, 16), t1, t_xm, t_zd, sig=False)
                if i % 2:
                    yield
            sc_t[n] = streams[f"scat{n % 2}"].token()

        done2 = attention(1, m, x2d, lambda b: x2_t[b], epi1, done1)
        m.free()

        m = Mem()
        WG = [m(f"WG{i}", [128, 3, 2, 256], F32) for i in range(4)]
        XE = [m(f"XE{i}", [80, 2, D], F32) for i in range(2)]
        XET = [m(f"XET{i}", [128, 2, C], F32) for i in range(2)]
        SI = [m(f"SI{i}", [128, 2, C], F32) for i in range(2)]
        HE = [m(f"HE{i}", [128, 2, C], F32) for i in range(2)]
        YE = [m(f"YE{i}", [80, 2, D], F32) for i in range(2)]
        t_gg = dve(lambda e: e.tensor_scalar(GG[:, :], GG[:, :], tg[:, 3:4], None, ALU.mult), done2)
        tk = {}

        def load_w(e_):
            for i, n in enumerate(("weg", "weu", "wed")):
                tk["w", e_] = dma(sp, f"we{e_ % 4}", WG[e_ % 4][:, i, :, :],
                                  a[n][e_].rearrange("(k p) n -> p k n", p=128), done2, tk.get(("y", e_ - 4)))

        def load_x(e_):
            tk["x", e_] = dma(sp, f"xe{e_ % 2}", XE[e_ % 2][:, :, :],
                              bufd[e_ * C:(e_ + 1) * C, :].rearrange("(t p) d -> p t d", p=80),
                              done2, tk.get(("xt", e_ - 2)))

        def turn(e_):
            bk = e_ % 2
            for kt in range(2):
                for st in range(2):
                    p = pe(lambda e, kt=kt, st=st: e.transpose(
                        PS[:, bk, 160 * kt + 80 * st:160 * kt + 80 * st + 80],
                        XE[e_ % 2][:, st, 128 * kt:128 * kt + 128], ident[0:80, 0:80]),
                        tk["x", e_], bank_free[bk], sig=(kt + st == 2))
            tk["xt", e_] = p
            bank_free[bk] = tk["xet", e_] = act(lambda e: e.activation(
                XET[e_ % 2][:, :, :], PS[:, bk, 0:320].rearrange("p (k n) -> p k n", k=2), ACT.Copy),
                p, tk.get(("gu", e_ - 2)))

        def gate_up(e_):
            for i in range(2):
                bk = 2 + 2 * (e_ % 2) + i
                for mt in range(2):
                    for k in range(2):
                        p = pe(lambda e, i=i, mt=mt, k=k, bk=bk: e.matmul(
                            PS[:, bk, 160 * mt:160 * mt + 160], WG[e_ % 4][:, i, k, 128 * mt:128 * mt + 128],
                            XET[e_ % 2][:, k, :], start=(k == 0), stop=(k == 1)),
                            tk["xet", e_], tk["w", e_], bank_free[bk], sig=(mt + k == 2))
                if i == 0:
                    ts = act(lambda e, bk=bk: e.activation(
                        SI[e_ % 2][:, :, :], PS[:, bk, 0:320].rearrange("p (k n) -> p k n", k=2), ACT.Silu),
                        p, tk.get(("h", e_ - 2)))
                    bank_free[bk] = ts
                else:
                    tk["gu", e_] = p
                    bank_free[bk] = tk["h", e_] = dve(lambda e, bk=bk: e.tensor_tensor(
                        HE[e_ % 2][:, :, :], PS[:, bk, 0:320].rearrange("p (k n) -> p k n", k=2),
                        SI[e_ % 2][:, :, :], ALU.mult), p, ts, tk.get(("y", e_ - 2)))

        def down(e_):
            bk = 6 + e_ % 2
            for st in range(2):
                for k in range(2):
                    p = pe(lambda e, st=st, k=k: e.matmul(
                        PS[0:80, bk, 256 * st:256 * st + 256], HE[e_ % 2][:, k, 80 * st:80 * st + 80],
                        WG[e_ % 4][:, 2, k, :], start=(k == 0), stop=(k == 1)),
                        tk["h", e_], bank_free[bk], sig=(st + k == 2))
            tk["y", e_] = p
            bank_free[bk] = t = dve(lambda e: e.tensor_copy(
                YE[e_ % 2][:, :, :], PS[0:80, bk, :].rearrange("p (t n) -> p t n", t=2)), p, tk.get(("yd", e_ - 2)))
            tk["yd", e_] = dma(sp, f"y{e_ % 2}", yd[e_ * C:(e_ + 1) * C, :].rearrange("(t p) d -> p t d", p=80),
                               YE[e_ % 2][:, :, :], t)

        for e_ in range(3):
            load_w(e_)
        load_x(0)
        load_x(1)
        turn(0)
        for e_ in range(E):
            if e_ + 2 < E:
                pass
            gate_up(e_)
            if e_ + 1 < E:
                turn(e_ + 1)
            if e_ + 2 < E:
                load_x(e_ + 2)
            if e_ + 3 < E:
                load_w(e_ + 3)
            down(e_)
        yt = [tk["yd", E - 1], tk["yd", E - 2]]
        NG = 8
        GT = [m(f"GT{i}", [128, D], F32) for i in range(NG)]
        fin = {}
        for n in range(32):
            name = f"gat{n % NG}"
            if name not in streams:
                streams[name] = Stream(sem("d_" + name))
            st_ = streams[name]
            st_.n += 16
            pool(lambda e, n=n, st_=st_: e.indirect_dma_start(
                out=GT[n % NG][:, :], out_offset=None, in_=yd,
                in_offset=bass.IndirectOffsetOnAxis(ap=SLG[:, n:n + 1], axis=0),
                bounds_check=EC - 1, oob_is_err=False).then_inc(st_.sem, 16), yt, done2, fin.get(n - NG), sig=False)
            t = dve(lambda e, n=n: e.scalar_tensor_tensor(
                BASE[:, n, :], GT[n % NG][:, :], GG[:, n:n + 1], BASE[:, n, :], ALU.mult, ALU.add),
                (st_.sem, st_.n), t_gg)
            fin[n] = t
            if n % 4 == 3:
                dma(sp, "out", a["out"][128 * (n - 3):128 * (n + 1), :].rearrange("(t p) d -> p t d", p=128),
                    BASE[:, n - 3:n + 1, :], t)
        m.free()
        top.free()
        fix.free()
        ends = [s.token() for s in streams.values()]

        for s, v in ends:
            nc.sync.wait_ge(s, v)


def _inputs(i):
    f = np.ascontiguousarray
    order = np.arange(256).reshape(16, 16).T.reshape(-1)
    out = {
        "x": f(i["x"].reshape(T, D)),
        "ctxT": f(i["ctx_1024"].reshape(T, D).T),
        "g_xattn": f(i["g_xattn"]), "g_ffn": f(i["g_ffn"]),
        "b0": f(i["L0_xattn_b_proj"]), "b1": f(i["L1_xattn_bo"]),
        "wup": f(i["L0_ffn_w_up"]), "wgate": f(i["L0_ffn_w_gate"]), "wdown": f(i["L0_ffn_w_down"]),
        "wr": f(i["L1_ffn_w_router"]), "weg": f(i["L1_ffn_w_gate"]), "weu": f(i["L1_ffn_w_up"]),
        "wed": f(i["L1_ffn_w_down"]),
    }
    mask = i["mask_Bx1xSxS2_bk0"].reshape(NB, S, S)
    out["mq"] = f(mask)
    out["mt"] = f(mask.transpose(0, 2, 1))
    for layer, names in enumerate((("L0_xattn_W_q", "L0_xattn_W_k", "L0_xattn_W_v", "L0_xattn_W_proj"),
                                   ("L1_xattn_Wq", "L1_xattn_Wk", "L1_xattn_Wv", "L1_xattn_Wo"))):
        for n, name in zip("qkvo", names):
            w = i[name]
            out[f"w{n}{layer}"] = f((w[order] if n in "qk" else w).T)
    return out


def kernel(**inputs):
    import concourse.bacc as bacc
    from concourse.bass_utils import run_bass_kernel_spmd

    nc = bacc.Bacc("TRN2", target_bir_lowering=False, num_devices=1)
    arrays, aps = {}, {}
    for name, arr in _inputs({k: np.asarray(v) for k, v in inputs.items()}).items():
        arrays["in_" + name] = arr
        aps[name] = nc.dram_tensor("in_" + name, arr.shape, mybir.dt.from_np(arr.dtype), kind="ExternalInput").ap()
    aps["out"] = nc.dram_tensor("out_0", (T, D), F32, kind="ExternalOutput").ap()
    build(nc, aps)
    r = run_bass_kernel_spmd(nc, [arrays], core_ids=[0])
    return r.results[0]["out_0"].reshape(NB, S, D)
```

```python
from contextlib import ExitStack

import numpy as np
import concourse.bass as bass
from concourse import mybir

F32 = mybir.dt.float32
BF16 = mybir.dt.bfloat16
F16 = mybir.dt.float16
I16 = mybir.dt.int16
U16 = mybir.dt.uint16
I32 = mybir.dt.int32
U8 = mybir.dt.uint8
ALU = mybir.AluOpType
ACT = mybir.ActivationFunctionType
X = mybir.AxisListType.X

NB, S, D, H, HD = 16, 256, 256, 16, 16
T = NB * S
FF = 768
E, C = 32, 160
EC = E * C
NEG = -1.0e10
EPS = 1e-5
QMAX = 32767.0


class Queue:

    def __init__(self, eng, sem):
        self.eng, self.sem, self.n, self.seen = eng, sem, 0, {}

    def __call__(self, fn, *waits, sig=True):
        need = {}
        for w in flat(waits):
            if self.seen.get(id(w[0]), 0) < w[1]:
                self.seen[id(w[0])] = w[1]
                need[id(w[0])] = w
        for s, v in need.values():
            self.eng.wait_ge(s, v)
        ins = fn(self.eng)
        if not sig:
            return None
        self.n += 1
        ins.then_inc(self.sem, 1)
        return (self.sem, self.n)

    def wait(self, *waits):
        for s, v in flat(waits):
            if self.seen.get(id(s), 0) < v:
                self.seen[id(s)] = v
                self.eng.wait_ge(s, v)

    def last(self):
        return (self.sem, self.n)


def flat(ws):
    for w in ws:
        if w is None:
            continue
        if isinstance(w, list):
            yield from flat(w)
        else:
            yield w


def bc(ap, axis, n):
    shape = list(ap.shape)
    return ap.unsqueeze(axis).broadcast_to(shape[:axis] + [n] + shape[axis:])


class Stream:

    def __init__(self, sem):
        self.sem, self.n = sem, 0

    def token(self):
        return (self.sem, self.n) if self.n else None


def build(nc, a):
    ctx = ExitStack()
    with ctx:
        def sem(name):
            return ctx.enter_context(nc.semaphore(name))

        def dram(name, shape, dt):
            return nc.dram_tensor(name, shape, dt).ap()

        pe, act, dve, pool, sp = (Queue(g, sem(n)) for g, n in (
            (nc.tensor, "s_pe"), (nc.scalar, "s_act"), (nc.vector, "s_dve"), (nc.gpsimd, "s_pool"), (nc.sync, "s_sp")))
        streams = {}

        def dma(q, name, out, in_, *waits, **kw):
            if name not in streams:
                streams[name] = Stream(sem("d_" + name))
            st = streams[name]
            st.n += 16
            q(lambda e, st=st: e.dma_start(out, in_, **kw).then_inc(st.sem, 16), *waits, sig=False)
            return (st.sem, st.n)

        x1d = dram("x1d", (T, D), F32)
        x2d = dram("x2d", (T, D), F32)
        qd = dram("qd", (3, 3, 256, 256), BF16)
        kd = dram("kd", (3, 3, 256, 256), BF16)
        bufd = dram("bufd", (EC, D + 2), F32)

        PS = ctx.enter_context(nc.psum_tensor("PS", [128, 8, 512], F32))
        bank_free = [None] * 8

        class Mem:

            count = 0

            def __init__(self):
                self.c = ExitStack()
                self.n = 0

            def __call__(self, name, shape, dt):
                Mem.count += 1
                return self.c.enter_context(nc.sbuf_tensor(f"{name}_{Mem.count}", shape, dt))

            def free(self):
                self.c.close()

        fix = Mem()
        ident = fix("ident", [128, 128], F32)
        identb = fix("identb", [128, 128], BF16)
        ones = fix("ones", [128, 128], F32)
        onesb = fix("onesb", [128, 128], BF16)
        triu = fix("triu", [128, 128], BF16)
        rev = fix("rev", [128, 8, 32], F32)
        gates = fix("gates", [128, 4], F32)
        tg = fix("tg", [128, 4], F32)
        bias_row = fix("bias_row", [128, 2, D], F32)
        tgb = fix("tgb", [128, 2, D], F32)
        mhalf = fix("mhalf", [128, 2], F32)
        sc = fix("sc", [128, 64], F32)
        wup = fix("wup", [128, 2, 2, FF], F16)
        wgt = fix("wgt", [128, 2, 2, FF], F16)
        wdn = fix("wdn", [128, 2, 6, D], F16)
        wsc = fix("wsc", [128, 3, 4], F32)
        XNT = fix("XNT", [128, 2, T], F32)
        XNf = XNT[:, :, :].rearrange("p k n -> p (k n)")
        PP = [fix(f"PP{i}", [128, 2, 3, 256], BF16) for i in range(2)]
        ST = [fix(f"ST{i}", [128, 32], F32) for i in range(2)]

        def piece(i):
            return XNf[:, 512 * i:512 * i + 512].rearrange("p (a n) -> p a n", a=2)

        t_wsc = {}

        t = [pool(lambda e, m=m, v=v: e.memset(m, v)) for m, v in (
            (ident[:, :], 0.0), (identb[:, :], 0.0), (ones[:, :], 1.0), (onesb[:, :], 1.0),
            (triu[:, :], 1.0), (mhalf[:, :], -0.5))]
        for m in (ident, identb):
            pool(lambda e, m=m: e.affine_select(out=m[:, :], in_=m[:, :], compare_op=ALU.not_equal, fill=1.0,
                                                base=0, pattern=[[-1, 128]], channel_multiplier=1), t)
        pool(lambda e: e.affine_select(out=triu[:, :], in_=triu[:, :], compare_op=ALU.is_ge, fill=0.0,
                                       base=0, pattern=[[1, 128]], channel_multiplier=-1), t)
        consts = pool(lambda e: e.iota(rev[:, :, :], pattern=[[0, 8], [-1, 32]], base=32, channel_multiplier=0,
                                       allow_small_or_imprecise_dtypes=True))
        g0 = dma(act, "g", gates[:, 0:2], a["g_xattn"].rearrange("(o n) -> o n", o=1).broadcast_to([128, 2]))
        g0 = dma(act, "g", gates[:, 2:4], a["g_ffn"].rearrange("(o n) -> o n", o=1).broadcast_to([128, 2]))
        g0 = dma(act, "g", bias_row[:, 0, :], a["b0"].rearrange("(o n) -> o n", o=1).broadcast_to([128, D]))
        g0 = dma(act, "g", bias_row[:, 1, :], a["b1"].rearrange("(o n) -> o n", o=1).broadcast_to([128, D]))
        t_tg = act(lambda e: e.activation(tg[:, :], gates[:, :], ACT.Tanh), g0)
        for i in range(2):
            t_tgb = pool(lambda e, i=i: e.tensor_scalar(tgb[:, i, :], bias_row[:, i, :], tg[:, i:i + 1], 0.0,
                                                        ALU.mult, ALU.add), t_tg, g0)

        def quantized_weights(m, bank):
            w = m("w_nat", [128, 1536], F32)
            q = m("w_q", [128, 512], I16)
            s = m("w_s", [128, 48], F32)
            r = m("w_r", [128, 48], F32)
            p = None
            for i, (n, dst, kt) in enumerate((("wup", wup, 2), ("wgate", wgt, 2), ("wdown", wdn, 6))):
                cols = 1536 // (kt * 128)
                ld = dma(sp, "wq", w[:, :].rearrange("p (m n) -> p m n", m=cols),
                         a[n].rearrange("(m p) n -> p m n", p=128), p, t_cr)
                yield from (None for _ in range(6))
                done = []
                for c in range(3):
                    f, g = slice(512 * c, 512 * c + 512), slice(16 * c, 16 * c + 16)
                    v = w[:, f].rearrange("p (b j) -> p b j", j=32)
                    t = dve(lambda e: e.tensor_reduce(s[:, g], v, X, ALU.max, apply_absolute_value=True), ld)
                    yield
                    t = dve(lambda e: e.tensor_scalar(s[:, g], s[:, g], 1.0 / 7.0, 1e-12, ALU.mult, ALU.max), t)
                    t = dve(lambda e: e.reciprocal(r[:, g], s[:, g]), t)
                    t = pool(lambda e: e.tensor_tensor(v, v, bc(r[:, g], 2, 32), ALU.mult), t)
                    yield from (None for _ in range(3))
                    t = dve(lambda e: e.tensor_scalar(q[:, :], w[:, f], 7.0, -8.0, ALU.min, ALU.max), t)
                    t = dve(lambda e: e.tensor_tensor(v, q[:, :].rearrange("p (b j) -> p b j", j=32),
                                                      bc(s[:, g], 2, 32), ALU.mult), t)
                    done.append(t)
                    yield
                t = dve(lambda e: e.tensor_reduce(wsc[:, i, 0:1], s[:, :], X, ALU.max), t)
                yield
                yield
                bk = bank()
                p = pe(lambda e: e.transpose(PS[0:1, bk, 0:128], wsc[:, i, 0:1], ident[:, :]), t, consts, bank_free[bk])
                bank_free[bk] = t = dve(lambda e: e.tensor_reduce(wsc[0:1, i, 1:2], PS[0:1, bk, 0:128], X, ALU.max), p)
                yield
                yield
                bk = bank()
                p = pe(lambda e: e.matmul(PS[:, bk, 0:1], ones[0:1, :], wsc[0:1, i, 1:2], start=True, stop=True),
                       t, bank_free[bk])
                bank_free[bk] = t = dve(lambda e: e.tensor_scalar(wsc[:, i, 2:3], PS[:, bk, 0:1], 7.0 / 16384.0, None,
                                                                  ALU.mult), p)
                t_wsc[i] = dve(lambda e: e.reciprocal(wsc[:, i, 3:4], wsc[:, i, 2:3]), t)
                for k in range(kt):
                    for mt in range(0, cols, 2):
                        yield
                        bk = bank()
                        for j in range(2):
                            src = w[:, (mt + j) * kt * 128 + k * 128:(mt + j) * kt * 128 + (k + 1) * 128]
                            p = pe(lambda e: e.transpose(PS[:, bk, 128 * j:128 * j + 128], src, ident[:, :]),
                                   done, consts, bank_free[bk])
                        hi, lo = (dst[:, j, k, mt * 128:(mt + 2) * 128] for j in range(2))
                        t = act(lambda e: e.activation(hi, PS[:, bk, 0:256], ACT.Copy, scale=wsc[:, i, 3:4]), p, t_wsc[i])
                        bank_free[bk] = dve(lambda e: e.scalar_tensor_tensor(
                            lo, PS[:, bk, 0:256], wsc[:, i, 3:4], hi, ALU.mult, ALU.subtract), t)

        def all_done():
            t = [q.last() for q in (pe, act, dve, pool) if q.n] + [s.token() for s in streams.values()]
            for q in (pe, act, dve, pool, sp):
                q.wait(t)
            return t

        scn = [0]

        def scalar_col(n=1):
            c = scn[0]
            scn[0] += n
            return c

        def global_scale(col, ncols, src, *waits):
            c = scalar_col(3)
            t = dve(lambda e: e.tensor_reduce(sc[:, c:c + 1], src, X, ALU.max, apply_absolute_value=True), *waits)
            p = pe(lambda e: e.transpose(PS[0:1, 7, 0:128], sc[:, c:c + 1], ident[:, :]), t, consts, bank_free[7])
            t = dve(lambda e: e.tensor_reduce(sc[0:1, c + 1:c + 2], PS[0:1, 7, 0:128], X, ALU.max), p)
            p = pe(lambda e: e.matmul(PS[:, 7, 128:129], ones[0:1, :], sc[0:1, c + 1:c + 2], start=True, stop=True), t)
            t = dve(lambda e: e.tensor_scalar(sc[:, c:c + 1], PS[:, 7, 128:129], 1.0 / QMAX, 1e-12,
                                              ALU.mult, ALU.max), p)
            bank_free[7] = t
            t = dve(lambda e: e.reciprocal(sc[:, c + 2:c + 3], sc[:, c:c + 1]), t)
            return sc[:, c:c + 1], sc[:, c + 2:c + 3], t

        crd = dram("crd", (8, 2048), F32)
        cr = XNf[0:64, 0:2048]
        pair = float(np.array([0x3F803F80], np.uint32).view(np.float32)[0])
        t = [dve(lambda e: e.memset(cr[0:32, :], pair)), dve(lambda e: e.memset(cr[32:33, :], 0.0))]
        dma(act, "cr", crd[0:4, :], cr[0:4, :], t)
        dma(act, "cr", crd[5:8, :], cr[5:8, :])
        t_cr = dma(act, "cr", crd[4:5, :], cr[32:33, :])

        def layer_norm(tag, x, out, st, t_x, nb, extra=None, free=None):
            for i in range(2):
                t = dve(lambda e, i=i: e.bn_stats(st[:, 16 + 6 * i:22 + 6 * i], x[:, i, :]), t_x, free)
            yield
            for i in range(2):
                t = dve(lambda e, i=i: e.bn_aggr(st[:, 2 * i:2 * i + 2], st[:, 16 + 6 * i:22 + 6 * i]), t)
            mv = st[:, 0:4].rearrange("p (t k) -> p t k", k=2)
            t1 = dve(lambda e: e.tensor_scalar(st[:, 4:6], mv[:, :, 0], -1.0, None, ALU.mult), t)
            t2 = dve(lambda e: e.tensor_scalar(st[:, 6:8], mv[:, :, 1], EPS, None, ALU.add), t)
            t = pool(lambda e: e.tensor_tensor(st[:, 8:10], st[:, 6:8], mhalf[:, :], ALU.pow), t2, consts)
            if extra is not None:
                t = pool(lambda e: e.tensor_tensor(st[:, 8:10], st[:, 8:10], extra[0], ALU.mult), t, extra[1])
            yield
            yield
            for i in range(2):
                t = dve(lambda e, i=i: e.tensor_scalar(out[:, i, :], x[:, i, :], st[:, 4 + i:5 + i],
                                                       st[:, 8 + i:9 + i], ALU.add, ALU.mult), t, t1, free)
                yield
            return t

        def attention(L, m, xin, t_xin, epilogue, keep):
            early = keep["early"]
            if L == 0:
                XB = [m(f"XB{i}", [128, 2, D], F32) for i in range(5)]
                XN = m("XN", [128, 2, D], F32)[:, :, :]
                XT = m("XT", [128, 2, 256], F32)[:, :, :]
                CT = [m(f"CT{i}", [128, 2, 256], F32) for i in range(2)]
                W = {n: m("W" + n, [128, 2, D], F32) for n in "qkvo"}
                QF = m("QF", [128, 2, 256], F32)[:, :, :]
                R1 = m("R1", [128, 2, 256], F32)[:, :, :]
            else:
                W = {n: piece(i) for i, n in enumerate("qkvo")}
                CT = [piece(4), piece(5)]
                XB = [piece(i) for i in (6, 7, 8, 13, 14)]
                XN, XT, QF, R1 = (piece(i) for i in (9, 10, 11, 12))
            t_w = {n: dma(sp, f"w{n}{L}", W[n][:, :, :], a[f"w{n}{L}"].rearrange("(k p) n -> p k n", p=128), early)
                   for n in "k"}
            ready = [False]
            init = []
            misc = [0]
            tok = {}
            live = []
            spawn = live.append

            def bank():
                misc[0] ^= 1
                return 6 + misc[0]

            def g(k, b):
                return tok.get((k, b))

            def put(k, b, v):
                tok[(k, b)] = v

            def load(b):
                assert b < 5 or (g("xfree", b - 5) and g("ctfree", b - 2))
                i = b % 5
                put("x", b, dma(sp, f"x{L}{i}", XB[i][:, :, :], xin[b * S:(b + 1) * S, :].rearrange(
                    "(t p) d -> p t d", p=128), early if b < 3 else keep, t_xin(b), g("xfree", b - 5)))
                j = b % 2
                put("ct", b, dma(sp, f"c{L}{j}", CT[j][:, :, :], a["ctxT"][:, b * S:(b + 1) * S].rearrange(
                    "(k p) n -> p k n", p=128), early, g("ctfree", b - 2)))
                if L == 0:
                    put("m", b, [dma(sp, f"m{j}", MQ[j][:, :, :], a["mq"][b].rearrange("(t p) n -> p t n", p=128),
                                     keep, g("mfree", b - 2)),
                                 dma(sp, f"m{j}", MT[j][:, :, :], a["mt"][b].rearrange("(t p) n -> p t n", p=128),
                                     keep, g("mfree", b - 2))])

            def gap(n):
                for _ in range(n):
                    yield

            def split(which, b, bk, p, scale):
                n = 0 if which == "q" else 1
                pp, r1 = PP[n], R1
                dd = (qd if which == "q" else kd)[b % 3]
                bankv = PS[:, bk, :].rearrange("p (m n) -> p m n", m=2)
                t1 = act(lambda e: e.activation(QF, bankv, ACT.Copy, scale=scale), p, g("r1", 0))
                th = act(lambda e: e.activation(pp[:, :, 0, :], bankv, ACT.Copy,
                                                scale=scale), g(which + "sent", b - 1))
                bank_free[bk] = th
                t = pool(lambda e: e.tensor_tensor(r1, QF, pp[:, :, 0, :], ALU.subtract), t1, th, g("lo", 0))
                put("r1", 0, t)
                yield from gap(2)
                t = dve(lambda e: e.tensor_copy(pp[:, :, 1, :], r1), t)
                t = pool(lambda e: e.tensor_tensor(pp[:, :, 2, :], r1, pp[:, :, 1, :], ALU.subtract), t)
                put("lo", 0, t)
                yield from gap(2)
                for part in range(3):
                    sent = dma(sp, f"{which}w", dd[part].rearrange("(m p) n -> p m n", p=128), pp[:, :, part, :],
                               t, g(which + "st", b - 3))
                put(which + "sent", b, sent)
                yield from gap(2)
                while not ready[0]:
                    yield
                st = (QS if which == "q" else KS)[b % 3]
                free = [g("c", b - 3), g("bdone", b - 3), init]
                flatd = dd.rearrange("s (r h) n -> s r (h n)", h=H)

                def stack(row, part, k=1):
                    dst = st[row:row + 16 * k, :, :].rearrange("p h n -> p (h n)")
                    src = flatd[part] if k == 1 else flatd[part:part + k].rearrange("s r n -> (s r) n")
                    return dma(sp, f"{which}s{b % 3}", dst, src, sent, free)

                if which == "q":
                    stack(0, 0, 3)
                    stack(48, 0, 2)
                    tt = stack(80, 0)
                else:
                    for s_, part in enumerate((0, 0, 0, 1, 1, 2)):
                        tt = stack(16 * s_, part)
                put(which + "st", b, tt)

            def project(w, src, bk, t):
                for mt in range(2):
                    for k in range(2):
                        p = pe(lambda e, mt=mt, k=k: e.matmul(
                            PS[:, bk, 256 * mt:256 * mt + 256], W[w][:, k, 128 * mt:128 * mt + 128], src[:, k, :],
                            start=(k == 0), stop=(k == 1)), t, t_w[w], bank_free[bk], sig=(mt + k == 2))
                return p

            def stN(b):
                j = b % 2
                ex = None
                if L == 0:
                    t = dve(lambda e: e.tensor_reduce(AV[j][:, :], MQ[j][:, :, :], X, ALU.max), g("m", b), g("xn", b - 2))
                    ex = (AV[j][:, :], t)
                    pool(lambda e: e.tensor_scalar(NQ[b % 4][:, :, :], MQ[j][:, :, :], -1.0, -NEG, ALU.add, ALU.mult),
                         g("m", b), g("bmax", b - 4))
                    tn = pool(lambda e: e.tensor_scalar(NK[b % 4][:, :, :], MT[j][:, :, :], -1.0, -NEG, ALU.add,
                                                        ALU.mult), g("c", b - 4))
                    put("mfree", b, [tn, t])
                    put("pen", b, tn)
                yield
                t = yield from layer_norm("a", XB[b % 5], XN, ST[j], g("x", b), b, ex, [g("xtr", b - 1), g("xn", b - 2)])
                put("xn", b, t)
                put("xb", b, pool(lambda e: e.tensor_tensor(
                    XB[b % 5][:, :, :], XB[b % 5][:, :, :], bc(tgb[:, L, :], 1, 2), ALU.add),
                    t, t_tgb))

            def stA(b):
                j = b % 2
                ct = CT[j]
                bk = bank()
                p = project("k", ct, bk, g("ct", b))
                spawn(split("k", b, bk, p, 1.0))
                t = g("xn", b)
                yield from gap(2)
                bk = bank()
                for kt in range(2):
                    for tt in range(2):
                        p = pe(lambda e, kt=kt, tt=tt: e.transpose(
                            PS[:, bk, 256 * kt + 128 * tt:256 * kt + 128 * tt + 128],
                            XN[:, tt, 128 * kt:128 * kt + 128], ident[:, :]), t, consts, bank_free[bk], sig=(kt + tt == 2))
                put("xtr", b, p)
                bank_free[bk] = t = act(lambda e: e.activation(
                    XT[:, :, :], PS[:, bk, :].rearrange("p (k n) -> p k n", k=2), ACT.Copy), p, g("qp", b - 1))
                yield from gap(2)
                bk = bank()
                p = project("q", XT, bk, t)
                put("qp", b, p)
                spawn(split("q", b, bk, p, 0.25))
                yield from gap(4)
                while not ready[0]:
                    yield
                bk = bank()
                for tt in range(2):
                    for k in range(2):
                        p = pe(lambda e, tt=tt, k=k: e.matmul(
                            PS[:, bk, 256 * tt:256 * tt + 256], ct[:, k, 128 * tt:128 * tt + 128], W["v"][:, k, :],
                            start=(k == 0), stop=(k == 1)), g("ct", b), t_w["v"], bank_free[bk], sig=(tt + k == 2))
                put("ctfree", b, p)
                bank_free[bk] = act(lambda e: e.activation(
                    V[b % 3][:, :, :, 0:16], PS[:, bk, :].rearrange("p (t h r) -> p t h r", t=2, h=H), ACT.Copy),
                    p, g("av", b - 3), init)
                put("v", b, bank_free[bk])

            def stB(b):
                Q, K = QS[b % 3], KS[b % 3]
                nm = NM[b % 2]
                for h in range(H):
                    bk = 2 + h % 2
                    for qt in range(2):
                        o = PS[:, bk, 256 * qt:256 * qt + 256]
                        p = pe(lambda e, o=o, h=h, qt=qt: e.matmul(
                            o, Q[0:96, h, 128 * qt:128 * qt + 128], K[0:96, h, :], start=True, stop=True),
                            g("qst", b), g("kst", b), bank_free[bk], sig=(qt == 1))
                    if L == 0:
                        for qt in range(2):
                            t = dve(lambda e: e.tensor_tensor_reduce(
                                MX[:, 2 * (h % 2) + qt, :], PS[:, bk, 256 * qt:256 * qt + 256], NQ[b % 4][:, qt, :], -1.0, 1.0e30,
                                ALU.add, ALU.min, nm[:, qt, h:h + 1]), p, g("pen", b), g("nm", b - 2), g("mx", 2 * (h % 2) + qt))
                            put("mx", 2 * (h % 2) + qt, t)
                        bank_free[bk] = t
                    else:
                        bank_free[bk] = dve(lambda e, h=h, bk=bk: e.tensor_reduce(
                            nm[:, :, h], PS[:, bk, :].rearrange("p (t n) -> p t n", t=2), X, ALU.max, negate=True),
                            p, g("nm", b - 2))
                    put("bmax", b, bank_free[bk])
                    if h == H - 1:
                        put("bdone", b, p)
                    if h % 8 == 7:
                        spawn(maxima(b, h // 8, bank_free[bk]))
                    yield

            def maxima(b, hh, t):
                Q, nm = QS[b % 3], NM[b % 2]
                v = nm[:, :, 8 * hh:8 * hh + 8]
                yield
                t = pool(lambda e: e.tensor_copy(NH[:, 0, :, :], v), t)
                pool(lambda e: e.tensor_copy(NP[:, :, 0, :], NH[:, 0, :, :]), t, g("ntr", 0))
                t = pool(lambda e: e.tensor_tensor(NR[:, :, :], v, NH[:, 0, :, :], ALU.subtract), t)
                t = pool(lambda e: e.tensor_copy(NH[:, 1, :, :], NR[:, :, :]), t)
                pool(lambda e: e.tensor_copy(NP[:, :, 1, :], NH[:, 1, :, :]), t)
                t = pool(lambda e: e.tensor_tensor(NP[:, :, 2, :], NR[:, :, :], NH[:, 1, :, :], ALU.subtract), t)
                if hh == 1:
                    put("nm", b, t)
                yield from gap(3)
                mb = bank()
                for qt in range(2):
                    p = pe(lambda e, qt=qt: e.transpose(
                        PS[0:24, mb, 128 * qt:128 * qt + 128],
                        NP[:, qt, :, :].rearrange("p a h -> p (a h)"), ident[:, :]),
                        t, consts, bank_free[mb], sig=(qt == 1))
                put("ntr", 0, p)
                nt = NT[hh]
                bank_free[mb] = t = act(lambda e: e.activation(nt[:, :], PS[0:24, mb, 0:256], ACT.Copy),
                                        p, g("nsent%d" % hh, 0))
                for part in range(3):
                    s = dma(sp, f"n{hh}{b % 3}", Q[97 + part:98 + part, 8 * hh:8 * hh + 8, :],
                            nt[8 * part:8 * part + 8, :], t, g("c", b - 3), init)
                put("nsent%d" % hh, 0, s)
                put("nst%d" % hh, b, s)

            def av(b, h):
                gi, i = h // 4, h % 4
                ob = 4 + h // 8
                for kt in range(2):
                    p = pe(lambda e, kt=kt: e.matmul(
                        PS[32 * i:32 * i + 32, ob, 256 * (gi % 2):256 * (gi % 2) + 256],
                        V[b % 3][:, kt, h, :], P[h % 4][:, kt, :], start=(kt == 0), stop=(kt == 1)),
                        g("p", (b, h)), g("v", b), bank_free[ob] if h % 8 == 0 else None, sig=(kt == 1))
                put("avp", h % 4, p)
                if h == H - 1:
                    put("av", b, p)
                if h % 8 == 7:
                    hh = h // 8
                    bank_free[ob] = act(lambda e: e.activation(
                        OT[b % 2][:, 2 * hh:2 * hh + 2, :], PS[:, ob, :].rearrange("p (g n) -> p g n", g=2), ACT.Copy),
                        p, g("otr", b - 2))
                    put("ot", b, bank_free[ob])

            def stC(b):
                Q, K = QS[b % 3], KS[b % 3]
                for h in range(H):
                    bk = h % 2
                    for kt in range(2):
                        o = PS[:, bk, 256 * kt:256 * kt + 256]
                        p = pe(lambda e, o=o, h=h, kt=kt: e.matmul(
                            o, K[0:100, h, 128 * kt:128 * kt + 128], Q[0:100, h, :], start=True, stop=(L == 1)),
                            g("nst%d" % (h // 8), b), bank_free[bk], sig=(L == 1 and kt == 1))
                        if L == 0:
                            p = pe(lambda e, o=o, kt=kt: e.matmul(o, identb[:, :], NK[b % 4][:, kt, :], start=False,
                                                                  stop=True), g("pen", b), sig=(kt == 1))
                    if h == H - 1:
                        put("c", b, p)
                    bank_free[bk] = act(lambda e, h=h, bk=bk: e.activation(
                        P[h % 4][:, :, :], PS[:, bk, :].rearrange("p (k n) -> p k n", k=2), ACT.Exp), p,
                        g("avp", h % 4))
                    put("p", (b, h), bank_free[bk])
                    if h >= 2:
                        av(b, h - 2)
                    yield

            def stD(b):
                av(b, H - 2)
                yield
                av(b, H - 1)
                yield from gap(2)
                for qt in range(2):
                    bk = bank()
                    for gi in range(4):
                        p = pe(lambda e, gi=gi, qt=qt, bk=bk: e.transpose(
                            PS[:, bk, 128 * gi:128 * gi + 128], OT[b % 2][:, gi, 128 * qt:128 * qt + 128],
                            ident[:, :]), g("ot", b), bank_free[bk], sig=(gi == 3))
                    pv = PS[:, bk, :].rearrange("p (h r) -> p h r", r=32)
                    t = dve(lambda e, qt=qt, pv=pv: e.reciprocal(RD[:, qt, :], pv[:, :, 16]), p)
                    bank_free[bk] = t = dve(lambda e, qt=qt, pv=pv: e.tensor_tensor(
                        ON[:, qt, :].rearrange("p (h r) -> p h r", r=16), pv[:, :, 0:16],
                        bc(RD[:, qt, :], 2, 16), ALU.mult), t, g("ontr", b - 1))
                    if qt == 1:
                        put("otr", b, p)
                    yield
                yield from gap(2)
                bk = bank()
                for kt in range(2):
                    for qt in range(2):
                        p = pe(lambda e, kt=kt, qt=qt: e.transpose(
                            PS[:, bk, 256 * kt + 128 * qt:256 * kt + 128 * qt + 128],
                            ON[:, qt, 128 * kt:128 * kt + 128], ident[:, :]), t, bank_free[bk], sig=(kt + qt == 2))
                put("ontr", b, p)
                bank_free[bk] = t = act(lambda e: e.activation(
                    ONT[:, :, :], PS[:, bk, :].rearrange("p (k n) -> p k n", k=2), ACT.Copy), p, g("op", b - 1))
                yield from gap(2)
                bk = bank()
                for qt in range(2):
                    for k in range(2):
                        p = pe(lambda e, qt=qt, k=k: e.matmul(
                            PS[:, bk, 256 * qt:256 * qt + 256], ONT[:, k, 128 * qt:128 * qt + 128],
                            W["o"][:, k, :], start=(k == 0), stop=(k == 1)), t, t_w["o"], bank_free[bk], sig=(qt + k == 2))
                put("op", b, p)
                xb = XB[b % 5]
                bank_free[bk] = t = dve(lambda e: e.scalar_tensor_tensor(
                    xb[:, :, :], PS[:, bk, :].rearrange("p (t n) -> p t n", t=2), tg[:, L:L + 1], xb[:, :, :],
                    ALU.mult, ALU.add), p, g("xb", b), t_tg)
                yield
                yield from epilogue(b, xb, t, bank, ST[b % 2], g, put)

            def slots():
                for s in range(-3, NB + 3):
                    if s == -3:
                        load(0)
                        for n in "qvo":
                            t_w[n] = dma(sp, f"w{n}{L}", W[n][:, :, :],
                                         a[f"w{n}{L}"].rearrange("(k p) n -> p k n", p=128), early)
                    if 0 <= s < NB:
                        spawn(stC(s))
                    if 0 <= s + 1 < NB:
                        spawn(stB(s + 1))
                    if 0 <= s + 2 < NB:
                        spawn(stA(s + 2))
                    if 0 <= s - 1 < NB:
                        spawn(stD(s - 1))
                    if L == 0 and s == 0:
                        spawn(quantized_weights(m, bank))
                    for slot in range(16 if s > -3 else 8):
                        if slot == 3 and 0 < s + 3 < NB:
                            load(s + 3)
                        if slot == (8 if s > -3 else 0) and 0 <= s + 3 < NB:
                            spawn(stN(s + 3))
                        live[:] = [x for x in live if next(x, "end") != "end"]
                        yield

            run = slots()
            if L == 1:
                for _ in range(20):
                    next(run)
                    yield
                yield "memory"
            keep = keep["late"]
            QS = [m(f"QS{i}", [100, H, 256], BF16) for i in range(3)]
            KS = [m(f"KS{i}", [100, H, 256], BF16) for i in range(3)]
            V = [m(f"V{i}", [128, 2, H, 32], F32) for i in range(3)]
            P = [m(f"P{i}", [128, 2, 256], F32) for i in range(4)]
            OT = [m(f"OT{i}", [128, 4, 256], F32) for i in range(2)]
            ON = m("ON", [128, 2, 256], F32)
            ONT = m("ONT", [128, 2, 256], F32)
            RD = m("RD", [128, 2, H], F32)
            NM = [m(f"NM{i}", [128, 2, H], F32) for i in range(2)]
            NH = m("NH", [128, 2, 2, 8], BF16)
            NR = m("NR", [128, 2, 8], F32)
            NP = m("NP", [128, 2, 3, 8], F32)
            NT = [m(f"NT{i}", [24, 256], BF16) for i in range(2)]
            if L == 0:
                MQ = [m(f"MQ{i}", [128, 2, 256], U8) for i in range(2)]
                MT = [m(f"MT{i}", [128, 2, 256], U8) for i in range(2)]
                AV = [m(f"AV{i}", [128, 2], F32) for i in range(2)]
                NQ = [m(f"NQ{i}", [128, 2, 256], BF16) for i in range(4)]
                MX = m("MX", [128, 4, 256], BF16)
                NK = [m(f"NK{i}", [128, 2, 256], BF16) for i in range(4)]
            for i in range(3):
                dma(sp, f"init{L}", QS[i][96:100, :, :].rearrange("p h n -> p (h n)").bitcast(F32), crd[0:4, :], keep, t_cr)
                t_ir = dma(sp, f"init{L}", KS[i][96:100, :, :].rearrange("p h n -> p (h n)").bitcast(F32), crd[4:8, :])
                t = pool(lambda e: e.memset(V[i][:, :, :, 16:32], 0.0), keep, t_cr)
                t_iv = pool(lambda e: e.memset(V[i][:, :, :, 16:17], 1.0), t)
            init[:] = [t_ir, t_iv]
            ready[0] = True
            yield from run
            assert not live

        top0 = Mem()
        AM = top0("AM", [128, 96], F32)
        m = Mem()
        XM = m("XM", [128, 2, D], F32)
        ST0 = m("ST0", [128, 32], F32)

        def epi0(b, xb, t, bank, st, g, put):
            put("x1", b, dma(sp, f"x1{b % 4}", x1d[b * S:(b + 1) * S, :].rearrange("(t p) d -> p t d", p=128),
                             xb[:, :, :], t))
            t = yield from layer_norm("e", xb, XM, ST0, t, b, None, [g("xmtr", b - 1), g("xm", b - 1)])
            put("xm", b, t)
            put("xfree", b, [t, g("x1", b)])
            for _ in range(2):
                yield
            bk = bank()
            for kt in range(2):
                for tt in range(2):
                    p = pe(lambda e, kt=kt, tt=tt: e.transpose(
                        PS[:, bk, 256 * kt + 128 * tt:256 * kt + 128 * tt + 128],
                        XM[:, tt, 128 * kt:128 * kt + 128], ident[:, :]), t, bank_free[bk], sig=(kt + tt == 2))
            put("xmtr", b, p)
            dst = XNT[:, :, b * S:(b + 1) * S]
            bank_free[bk] = t = act(lambda e: e.activation(
                dst, PS[:, bk, :].rearrange("p (k n) -> p k n", k=2), ACT.Copy), p, t_cr)
            yield
            yield
            t_am[0] = dve(lambda e: e.tensor_reduce(AM[:, b:b + 1], dst, mybir.AxisListType.XY, ALU.max,
                                                    apply_absolute_value=True), t)
            x1_t[b] = g("x1", b)
            yield

        t_am, x1_t = [None], {}
        for _ in attention(0, m, a["x"], lambda b: None, epi0, {"early": None, "late": None}):
            pass
        done0 = all_done()
        m.free()

        m = Mem()
        G = m("G", [128, 6, T], F32)
        UQ = m("UQ", [128, 6, T], I16)
        Gf = G[:, :, :].rearrange("p m n -> p (m n)")
        UQf = UQ[:, :, :].rearrange("p m n -> p (m n)")
        s1, i1, t = global_scale(0, 16, AM[:, 0:16], t_am[0])
        zero_row = bias_row[:, :, :].rearrange("p i n -> p (i n)")[:, 0:D + 2]
        t_z = pool(lambda e: e.memset(zero_row, 0.0), t_tgb)
        for i in range(EC // 128 // 8):
            t_zd = dma(sp, "zero", bufd[1024 * i:1024 * i + 1024, :].rearrange("(t p) d -> p t d", p=128),
                       bc(zero_row, 1, 8), t_z)
        PARTS = ((0, 0), (0, 1), (1, 0))
        XH = XNT[:, :, :].bitcast(F16)
        tq, tqi = {}, {}
        for n in range(9):
            if n < 8:
                tqi[n] = dve(lambda e: e.tensor_scalar(UQ[:, 0:2, 512 * n:512 * n + 512], XNT[:, :, 512 * n:512 * n + 512],
                                                       i1, QMAX, ALU.mult, ALU.min), t, done0)
            if n:
                hi, lo = (XH[:, :, 1024 * n - 1024 + 512 * j:1024 * n - 512 + 512 * j] for j in range(2))
                q = UQ[:, 0:2, 512 * n - 512:512 * n]
                th = act(lambda e: e.activation(hi, q, ACT.Copy), tqi[n - 1])
                tq[n - 1] = dve(lambda e: e.tensor_tensor(lo, q, hi, ALU.subtract), th)
        us = scalar_col(2)
        us, gs = sc[:, us:us + 1], sc[:, us + 1:us + 2]
        t_us = dve(lambda e: e.tensor_tensor(us, s1, wsc[:, 0, 2:3], ALU.mult), t)
        t_us = dve(lambda e: e.tensor_tensor(gs, s1, wsc[:, 1, 2:3], ALU.mult), t)

        def ff_in(w, scale, wait, col):
            out = None
            for n in range(8):
                for mt in range(6):
                    bk = (n * 6 + mt) % 7
                    for j, (wp, xp) in enumerate(PARTS * 2):
                        k = j // 3
                        p = pe(lambda e: e.matmul(
                            PS[:, bk, :], w[:, wp, k, 128 * mt:128 * mt + 128],
                            XH[:, k, 1024 * n + 512 * xp:1024 * n + 512 * xp + 512],
                            start=(j == 0), stop=(j == 5)), tq[n], bank_free[bk], sig=(j == 5))
                    dst = G[:, mt, 512 * n:512 * n + 512]
                    bank_free[bk] = t = act(lambda e: e.activation(dst, PS[:, bk, :], ACT.Copy, scale=scale), p,
                                            t_us, wait(mt, n))
                    c = n * 6 + mt
                    out = dve(lambda e, dst=dst, c=c: e.tensor_reduce(
                        AM[:, col + c:col + c + 1], dst, X, ALU.max, apply_absolute_value=True), t)
            return out

        t = ff_in(wup, us, lambda mt, n: None, 48 * 0)
        s2, i2, t = global_scale(0, 48, AM[:, 0:48], t)
        tu = {}
        for n in range(8):
            v, q = G[:, :, 512 * n:512 * n + 512], UQ[:, :, 512 * n:512 * n + 512]
            tu[n] = dve(lambda e, v=v, q=q: e.tensor_scalar(q, v, i2, QMAX, ALU.mult, ALU.min), t, tq[7])
        t = ff_in(wgt, gs, lambda mt, n: tu[n], 48)
        s3, i3, t = global_scale(0, 48, AM[:, 48:96], t)
        NCH = 24
        CW = 6 * T // NCH
        GQ = [XNf[:, 512 * i:512 * i + 512].bitcast(I16) for i in range(3)]
        SG = [XNf[:, 1536 + 1024 * i:2560 + 1024 * i] for i in range(3)]
        SQ = [XNf[:, 4608 + 512 * i:5120 + 512 * i].bitcast(U16) for i in range(3)]
        t0, tsg, tsq, tgs = t, {}, {}, {}
        for c in range(NCH + 3):
            if c < NCH:
                v = Gf[:, CW * c:CW * c + CW]
                t = act(lambda e: e.activation(GQ[c % 3], v, ACT.Copy, scale=i3), t0, pe.last(), tgs.get(c - 3))
                tsg[c] = act(lambda e: e.activation(SG[c % 3], GQ[c % 3], ACT.Sigmoid, scale=s3), t, tsq.get(c - 3))
            k = c - 1
            if 0 <= k < NCH:
                tsq[k] = pool(lambda e: e.tensor_scalar(SQ[k % 3], SG[k % 3], 65536.0, 0.0, ALU.mult, ALU.add),
                              tsg[k], tgs.get(k - 3))
            k = c - 2
            if 0 <= k < NCH:
                v = Gf[:, CW * k:CW * k + CW]
                tgs[k] = dve(lambda e: e.tensor_tensor_reduce(v, GQ[k % 3], SQ[k % 3], s3, -1.0e30, ALU.mult, ALU.max,
                                                              AM[:, k:k + 1]), tsq[k])
            k = c - 3
            if 0 <= k < NCH:
                v = Gf[:, CW * k:CW * k + CW]
                t = dve(lambda e: e.tensor_scalar(v, v, 1.0, None, ALU.mult, ALU.min, accum_out=AM[:, 24 + k:25 + k]),
                        tgs[k])
        s4, i4, t0 = global_scale(0, NCH, AM[:, 0:2 * NCH], t)
        tgq, tpr = {}, {}
        for c in range(NCH + 2):
            if c < NCH:
                v = Gf[:, CW * c:CW * c + CW]
                tgq[c] = act(lambda e: e.activation(GQ[c % 3], v, ACT.Copy, scale=i4), t0, tpr.get(c - 3))
            k = c - 1
            if 0 <= k < NCH:
                v, u = Gf[:, CW * k:CW * k + CW], UQf[:, CW * k:CW * k + CW]
                tpr[k] = dve(lambda e: e.tensor_tensor_reduce(v, GQ[k % 3], u, 1.0, -1.0e30, ALU.mult, ALU.max,
                                                              AM[:, 48 + k:49 + k]), tgq[k])
            k = c - 2
            if 0 <= k < NCH:
                v = Gf[:, CW * k:CW * k + CW]
                t = dve(lambda e: e.tensor_scalar(v, v, 1.0, None, ALU.mult, ALU.min, accum_out=AM[:, 72 + k:73 + k]),
                        tpr[k])
        s5, i5, t = global_scale(0, NCH, AM[:, 48:48 + 2 * NCH], t)
        c = scalar_col(2)
        fs = sc[:, c:c + 1]
        t5 = dve(lambda e: e.tensor_scalar(fs, s5, s4, s2, ALU.mult, ALU.mult), t)
        t5 = dve(lambda e: e.tensor_scalar(fs, fs, tg[:, 2:3], 1.0 / 65536.0, ALU.mult, ALU.mult), t5)
        t5 = dve(lambda e: e.tensor_tensor(fs, fs, wsc[:, 2, 2:3], ALU.mult), t5)
        XD = [piece(13 + i) for i in range(3)]
        x2_t = {}
        stt, tin, ld = {}, {}, {}

        GH = G[:, :, :].bitcast(F16)
        t_q = {}

        def down_quant(b):
            t_q[b] = dve(lambda e: e.tensor_scalar(UQ[:, :, 256 * b:256 * b + 256], G[:, :, 256 * b:256 * b + 256],
                                                   i5, QMAX, ALU.mult, ALU.min), t)

        def down_in(b):
            q = UQ[:, :, 256 * b:256 * b + 256]
            hi, lo = (GH[:, :, 512 * b + 256 * j:512 * b + 256 * j + 256] for j in range(2))
            t1 = act(lambda e: e.activation(hi, q, ACT.Copy), t_q[b])
            if b + 1 < NB:
                down_quant(b + 1)
            tin[b] = dve(lambda e: e.tensor_tensor(lo, q, hi, ALU.subtract), t1)
            ld[b] = dma(sp, f"xd{b % 3}", XD[b % 3], x1d[b * S:(b + 1) * S, :].rearrange(
                "(t p) d -> p t d", p=128), x1_t[b], stt.get(b - 3), t)

        keep1 = {"early": t5}
        top = Mem()
        m1 = Mem()
        att1 = attention(1, m1, x2d, lambda b: x2_t[b], lambda *v: epi1(*v), keep1)
        down_quant(0)
        down_in(0)
        down_in(1)
        for b in range(NB):
            if b + 2 < NB:
                down_in(b + 2)
            bk = b % 6
            for tt in range(2):
                for j, (wp, xp) in enumerate(((0, 0), (1, 0), (0, 1)) * 6):
                    k = j // 3
                    c = 512 * b + 256 * xp + 128 * tt
                    p = pe(lambda e: e.matmul(
                        PS[:, bk, 256 * tt:256 * tt + 256], GH[:, k, c:c + 128], wdn[:, wp, k, :],
                        start=(j == 0), stop=(j == 17)), tin[b], bank_free[bk], sig=(tt == 1 and j == 17))
            bank_free[bk] = t2 = dve(lambda e: e.scalar_tensor_tensor(
                XD[b % 3], PS[:, bk, :].rearrange("p (t n) -> p t n", t=2), fs, XD[b % 3],
                ALU.mult, ALU.add), p, ld[b], t5)
            stt[b] = x2_t[b] = dma(sp, f"x2{b % 3}", x2d[b * S:(b + 1) * S, :].rearrange("(t p) d -> p t d", p=128),
                                   XD[b % 3], t2)
            if 3 <= b < 13:
                next(att1)
                next(att1)
        assert next(att1) == "memory"
        done1 = keep1["late"] = all_done()
        m.free()
        top0.free()

        SLS = top("SLS", [128, 32], I32)
        WG = [top(f"WG{i}", [128, 3, 2, 256], F32) for i in range(4)]
        tk = {}

        def load_w(e_, *waits):
            for i, n in enumerate(("weg", "weu", "wed")):
                tk["w", e_] = dma(sp, f"we{e_ % 4}", WG[e_ % 4][:, i, :, :],
                                  a[n][e_].rearrange("(k p) n -> p k n", p=128), *waits, tk.get(("y", e_ - 4)))

        m = m1
        XMS = m("XM1", [128, 2, 8, D + 2], F32)
        NUM = m("NUM", [128, 32], F32)
        ST0 = m("ST1", [128, 32], F32)
        XMT = m("XMT", [128, 2, 256], F32)
        WR = m("WR", [128, 2, E], F32)
        LG = m("LG", [128, 2, 8, E], F32)
        EX = m("EX", [128, 8, E], F32)
        OHF = m("OHF", [128, 8, E], F32)
        OHB = m("OHB", [128, 8, E], BF16)
        CN = m("CN", [128, 2, E], BF16)
        CS = m("CS", [128, E], F32)
        RS = m("RS", [128, 8, 8], F32)
        t_num = pool(lambda e: e.iota(NUM[:, :], pattern=[[128, 32]], base=1, channel_multiplier=1,
                                      allow_small_or_imprecise_dtypes=True), done1)
        t_c = dve(lambda e: e.memset(CN[:, :, :], 0.0), done1)
        t_wr = dma(sp, "wr", WR[:, :, :], a["wr"].rearrange("(k p) n -> p k n", p=128), done1)
        cn_t = [t_c]
        sc_t = {}
        rt_t = {}
        for i in range(2):
            streams[f"scat{i}"] = Stream(sem(f"d_scat{i}"))
        groups = [(0, 4), (4, 4), (8, 4), (12, 3), (15, 1)]
        group_of = {b: (n, b - b0, nb) for n, (b0, nb) in enumerate(groups) for b in range(b0, b0 + nb)}

        t_base = [None]

        def epi1(b, xb, t, bank, st, g, put):
            n, at, nb = group_of[b]
            if b < 3:
                load_w(b, done1)
            XM = XMS[:, n % 2, 2 * at:2 * at + 2, 0:D]
            t = yield from layer_norm("e", xb, XM, ST0, t, b, None, [g("xm", b - 1), sc_t.get(n - 2)])
            put("xm", b, t)
            yield
            tb = dve(lambda e: e.scalar_tensor_tensor(xb[:, :, :], XM, tg[:, 3:4], xb[:, :, :], ALU.mult, ALU.add), t)
            t_base[0] = dma(sp, "base", a["out"][b * S:(b + 1) * S, :].rearrange("(t p) d -> p t d", p=128),
                            xb[:, :, :], tb)
            put("xfree", b, [t, t_base[0]])
            yield
            bk = bank()
            for kt in range(2):
                for tt in range(2):
                    p = pe(lambda e, kt=kt, tt=tt: e.transpose(
                        PS[:, bk, 256 * kt + 128 * tt:256 * kt + 128 * tt + 128],
                        XM[:, tt, 128 * kt:128 * kt + 128], ident[:, :]), t, bank_free[bk], sig=(kt + tt == 2))
            bank_free[bk] = t = act(lambda e: e.activation(
                XMT[:, :, :], PS[:, bk, :].rearrange("p (k n) -> p k n", k=2), ACT.Copy), p, g("rt", b - 1))
            yield
            yield
            bk = bank()
            for tt in range(2):
                for kt in range(2):
                    p = pe(lambda e, kt=kt, tt=tt: e.matmul(
                        PS[:, bk, 32 * tt:32 * tt + 32], XMT[:, kt, 128 * tt:128 * tt + 128], WR[:, kt, :],
                        start=(kt == 0), stop=(kt == 1)), t, t_wr, bank_free[bk], sig=(kt + tt == 2))
            put("rt", b, p)
            bank_free[bk] = act(lambda e: e.activation(
                LG[:, n % 2, 2 * at:2 * at + 2, :], PS[:, bk, 0:64].rearrange("p (t n) -> p t n", t=2), ACT.Copy),
                p, rt_t.get(n - 2))
            if at == nb - 1:
                t = bank_free[bk]
                yield
                yield from route(n, t, [g("xm", k) for k in range(b - at, b + 1)], bank)

        def route(n, t, t_xm, bank):
            b0, nb = groups[n]
            w = 2 * nb
            lg = LG[:, n % 2, 0:w, :]
            ex, ohf, ohb, rs = EX[:, 0:w, :], OHF[:, 0:w, :], OHB[:, 0:w, :], RS[:, :, 0:w]
            mx, sm, rv, ps, sl, ac = (rs[:, i, :] for i in range(6))
            t = dve(lambda e: e.tensor_reduce(mx, lg, X, ALU.max), t, rt_t.get(n - 1))
            t = dve(lambda e: e.tensor_tensor(ohf, lg, bc(mx, 2, E), ALU.subtract), t)
            te = act(lambda e: e.activation(ex, ohf, ACT.Exp), t)
            yield
            t = dve(lambda e: e.tensor_reduce(sm, ex, X, ALU.add), te)
            t_sm = dve(lambda e: e.reciprocal(sm, sm), t)
            t = dve(lambda e: e.scalar_tensor_tensor(ex, ohf, 0.0, rev[:, 0:w, :], ALU.is_equal, ALU.mult), t)
            t = dve(lambda e: e.tensor_reduce(rv, ex, X, ALU.max), t)
            t = dve(lambda e: e.tensor_tensor(ohb, rev[:, 0:w, :], bc(rv, 2, E), ALU.is_equal), t)
            tc = dve(lambda e: e.tensor_reduce(CS[:, :], ohb.rearrange("p t n -> p n t"), X, ALU.add), t)
            tc = dve(lambda e: e.tensor_tensor(CN[:, (n + 1) % 2, :], CN[:, n % 2, :], CS[:, :], ALU.add), tc, cn_t[0])
            cn_t0, cn_t[0] = cn_t[0], tc
            yield
            yield
            bk = bank()
            o = PS[:, bk, 0:32 * w].rearrange("p (t n) -> p t n", n=E)
            pe(lambda e: e.matmul(o, triu[:, :], ohb, start=True, stop=False), t, bank_free[bk], sig=False)
            for j in range(w - 1):
                pe(lambda e: e.matmul(o[:, j + 1:w, :], onesb[:, :], bc(ohb[:, j, :], 1, w - 1 - j),
                                      start=False, stop=False), sig=False)
            p = pe(lambda e: e.matmul(o, onesb[:, :], bc(CN[:, n % 2, :], 1, w), start=False, stop=True), cn_t0)
            bank_free[bk] = t = dve(lambda e: e.tensor_tensor(ohf, o, ohb, ALU.mult), p)
            t = dve(lambda e: e.tensor_reduce(ps, ohf, X, ALU.add), t)
            t = dve(lambda e: e.tensor_scalar(sl, rv, -float(C), float(C * E - 1), ALU.mult, ALU.add), t)
            ta = dve(lambda e: e.tensor_scalar(ac, ps, float(C), None, ALU.is_le), t)
            t = dve(lambda e: e.tensor_tensor(sl, sl, ps, ALU.add), t)
            t = dve(lambda e: e.tensor_tensor(sl, sl, ac, ALU.mult), t, ta)
            xms = XMS[:, n % 2, 0:w, :]
            tx = dve(lambda e: e.tensor_scalar(xms[:, :, D + 1], sm, tg[:, 3:4], None, ALU.mult), t_sm, sc_t.get(n - 2))
            tx = dve(lambda e: e.tensor_copy(xms[:, :, D], NUM[:, 2 * b0:2 * b0 + w]), t_num)
            t1 = dve(lambda e: e.tensor_scalar(ac, ac, -1.0e6, 1.0e6, ALU.mult, ALU.add), t)
            t1 = dve(lambda e: e.tensor_tensor(SLS[:, 2 * b0:2 * b0 + w], sl, ac, ALU.add), t1)
            rt_t[n] = t1
            for i in range(w):
                st_ = streams[f"scat{n % 2}"]
                st_.n += 16
                pool(lambda e: e.indirect_dma_start(
                    out=bufd, out_offset=bass.IndirectOffsetOnAxis(ap=SLS[:, 2 * b0 + i:2 * b0 + i + 1], axis=0),
                    in_=XMS[:, n % 2, i, :], in_offset=None, bounds_check=EC - 1,
                    oob_is_err=False).then_inc(st_.sem, 16), t1, t_xm, tx, t_zd, sig=False)
                yield
            sc_t[n] = streams[f"scat{n % 2}"].token()

        for _ in att1:
            pass
        done2 = all_done()
        m.free()

        m = Mem()
        XE = [m(f"XE{i}", [80, 2, D + 2], F32) for i in range(4)]
        IX = [m(f"IX{i}", [80, 4], F32) for i in range(4)]
        IT = [m(f"IT{i}", [80, 2], I32) for i in range(4)]
        XET = [m(f"XET{i}", [128, 2, C], F32) for i in range(2)]
        SI = [m(f"SI{i}", [128, 2, C], F32) for i in range(2)]
        HE = [m(f"HE{i}", [128, 2, C], F32) for i in range(2)]
        YE = [m(f"YE{i}", [80, 2, D], F32) for i in range(4)]
        for i in range(4):
            streams[f"y{i}"] = Stream(sem(f"d_y{i}"))

        def load_x(e_):
            tk["x", e_] = dma(sp, f"xe{e_ % 4}", XE[e_ % 4][:, :, :],
                              bufd[e_ * C:(e_ + 1) * C, :].rearrange("(t p) d -> p t d", p=80),
                              done2, tk.get(("xt", e_ - 4)), tk.get(("yt", e_ - 4)))

        def turn(e_):
            bk = e_ % 2
            for kt in range(2):
                for st in range(2):
                    p = pe(lambda e, kt=kt, st=st: e.transpose(
                        PS[:, bk, 160 * kt + 80 * st:160 * kt + 80 * st + 80],
                        XE[e_ % 4][:, st, 128 * kt:128 * kt + 128], ident[0:80, 0:80]),
                        tk["x", e_], bank_free[bk], sig=(kt + st == 2))
            tk["xt", e_] = p
            bank_free[bk] = tk["xet", e_] = act(lambda e: e.activation(
                XET[e_ % 2][:, :, :], PS[:, bk, 0:320].rearrange("p (k n) -> p k n", k=2), ACT.Copy),
                p, tk.get(("gu", e_ - 2)))

        def gate_up(e_):
            for i in range(2):
                bk = 2 + 2 * (e_ % 2) + i
                for mt in range(2):
                    for k in range(2):
                        p = pe(lambda e, i=i, mt=mt, k=k, bk=bk: e.matmul(
                            PS[:, bk, 160 * mt:160 * mt + 160], WG[e_ % 4][:, i, k, 128 * mt:128 * mt + 128],
                            XET[e_ % 2][:, k, :], start=(k == 0), stop=(k == 1)),
                            tk["xet", e_], tk["w", e_], bank_free[bk], sig=(mt + k == 2))
                if i == 0:
                    ts = act(lambda e, bk=bk: e.activation(
                        SI[e_ % 2][:, :, :], PS[:, bk, 0:320].rearrange("p (k n) -> p k n", k=2), ACT.Silu),
                        p, tk.get(("h", e_ - 2)))
                    bank_free[bk] = ts
                else:
                    tk["gu", e_] = p
                    bank_free[bk] = tk["h", e_] = dve(lambda e, bk=bk: e.tensor_tensor(
                        HE[e_ % 2][:, :, :], PS[:, bk, 0:320].rearrange("p (k n) -> p k n", k=2),
                        SI[e_ % 2][:, :, :], ALU.mult), p, ts, tk.get(("y", e_ - 2)))

        def down(e_):
            bk = 6 + e_ % 2
            for st in range(2):
                for k in range(2):
                    p = pe(lambda e, st=st, k=k: e.matmul(
                        PS[0:80, bk, 256 * st:256 * st + 256], HE[e_ % 2][:, k, 80 * st:80 * st + 80],
                        WG[e_ % 4][:, 2, k, :], start=(k == 0), stop=(k == 1)),
                        tk["h", e_], bank_free[bk], sig=(st + k == 2))
            tk["y", e_] = p
            xe, ix, it, ye = XE[e_ % 4], IX[e_ % 4], IT[e_ % 4], YE[e_ % 4]
            t = dve(lambda e: e.tensor_scalar(ix[:, 0:2], xe[:, :, D], 0.0, 1.0e6, ALU.is_equal, ALU.mult), tk["x", e_],
                    tk.get(("i", e_ - 4)))
            tk["i", e_] = t = dve(lambda e: e.scalar_tensor_tensor(it[:, :], xe[:, :, D], -1.0, ix[:, 0:2], ALU.add,
                                                                   ALU.add), t, tk.get(("yd", e_ - 4)))
            for st in range(2):
                ty = dve(lambda e: e.tensor_scalar(ye[:, st, :], PS[0:80, bk, 256 * st:256 * st + 256],
                                                   xe[:, st, D + 1:D + 2], None, ALU.mult), p, tk.get(("yd", e_ - 4)))
            bank_free[bk] = tk["yt", e_] = ty
            for st in range(2):
                sy = streams[f"y{e_ % 4}"]
                sy.n += 16
                pool(lambda e: e.indirect_dma_start(
                    out=a["out"], out_offset=bass.IndirectOffsetOnAxis(ap=it[:, st:st + 1], axis=0),
                    in_=ye[:, st, :], in_offset=None, bounds_check=T - 1, oob_is_err=False,
                    compute_op=ALU.add).then_inc(sy.sem, 16), ty, t, t_base[0], sig=False)
            tk["yd", e_] = sy.token()

        load_x(0)
        load_x(1)
        load_x(2)
        turn(0)
        for e_ in range(E):
            gate_up(e_)
            if e_ + 1 < E:
                turn(e_ + 1)
            if e_ + 3 < E:
                load_x(e_ + 3)
            if e_ + 3 < E:
                load_w(e_ + 3)
            down(e_)
        m.free()
        top.free()
        fix.free()
        ends = [s.token() for s in streams.values()]

        for s, v in ends:
            nc.sync.wait_ge(s, v)


def _inputs(i):
    f = np.ascontiguousarray
    order = np.arange(256).reshape(16, 16).T.reshape(-1)
    out = {
        "x": f(i["x"].reshape(T, D)),
        "ctxT": f(i["ctx_1024"].reshape(T, D).T),
        "g_xattn": f(i["g_xattn"]), "g_ffn": f(i["g_ffn"]),
        "b0": f(i["L0_xattn_b_proj"]), "b1": f(i["L1_xattn_bo"]),
        "wup": f(i["L0_ffn_w_up"]), "wgate": f(i["L0_ffn_w_gate"]), "wdown": f(i["L0_ffn_w_down"]),
        "wr": f(i["L1_ffn_w_router"]), "weg": f(i["L1_ffn_w_gate"]), "weu": f(i["L1_ffn_w_up"]),
        "wed": f(i["L1_ffn_w_down"]),
    }
    mask = i["mask_Bx1xSxS2_bk0"].reshape(NB, S, S)
    out["mq"] = f(mask)
    out["mt"] = f(mask.transpose(0, 2, 1))
    for layer, names in enumerate((("L0_xattn_W_q", "L0_xattn_W_k", "L0_xattn_W_v", "L0_xattn_W_proj"),
                                   ("L1_xattn_Wq", "L1_xattn_Wk", "L1_xattn_Wv", "L1_xattn_Wo"))):
        for n, name in zip("qkvo", names):
            w = i[name]
            out[f"w{n}{layer}"] = f((w[order] if n in "qk" else w).T)
    return out


def kernel(**inputs):
    import concourse.bacc as bacc
    from concourse.bass_utils import run_bass_kernel_spmd

    nc = bacc.Bacc("TRN2", target_bir_lowering=False, num_devices=1)
    arrays, aps = {}, {}
    for name, arr in _inputs({k: np.asarray(v) for k, v in inputs.items()}).items():
        arrays["in_" + name] = arr
        aps[name] = nc.dram_tensor("in_" + name, arr.shape, mybir.dt.from_np(arr.dtype), kind="ExternalInput").ap()
    aps["out"] = nc.dram_tensor("out_0", (T, D), F32, kind="ExternalOutput").ap()
    build(nc, aps)
    r = run_bass_kernel_spmd(nc, [arrays], core_ids=[0])
    return r.results[0]["out_0"].reshape(NB, S, D)
```
